# Optimizing a Trainium2 kernel written in Bass

```python
import numpy as np
import jax
import jax.numpy as jnp

def _softmax(x, axis=-1):
    return jax.nn.softmax(x, axis=axis)

def _gelu(x):
    return jax.nn.gelu(x, approximate=True)

def _silu(x):
    return jax.nn.silu(x)

def _sigmoid(x):
    return jax.nn.sigmoid(x)

def _layernorm(x, axis=-1, eps=1e-05):
    m = jnp.mean(x, axis=axis, keepdims=True)
    v = jnp.var(x, axis=axis, keepdims=True)
    return (x - m) / jnp.sqrt(v + eps)

def _scatter_add(tgt, idx, src, axis=0):
    return tgt.at[idx].add(src)

def _segment_sum(src, seg, n):
    return jax.ops.segment_sum(src, seg, n)
kernel_name = 'mk_adj_resnorm_d2_adj_r2_981c21'

def setup_inputs(seed: int=0):
    np.random.seed(seed)
    _w = jnp.asarray

    def _rec_inputs():
        import jax
        import jax.numpy as jnp
        _gk = jax.random.key(seed)
        x = -0.0002928 + 1 * jax.random.normal(jax.random.fold_in(_gk, 1), (4096, 256), jnp.float32)
        _a = jax.random.bernoulli(jax.random.fold_in(_gk, 2), 0.00195312, (4096, 4096))
        _a = jnp.logical_or(_a, jnp.eye(4096, dtype=bool))
        _af = _a.astype(jnp.float32)
        _af = _af * jax.random.uniform(jax.random.fold_in(_gk, 3), (4096, 4096), jnp.float32, 0.05, 1)
        adj = _af
        return (x, adj)
    x, adj = _rec_inputs()

    def _L0_gnn_setup():
        import jax, jax.numpy as jnp
        import numpy as np
        N_NODES = 4096
        DIM = 256
        key = jax.random.key(seed)
        k1, k2, k3, k4 = jax.random.split(key, 4)
        x = jax.random.normal(k1, (N_NODES, DIM), dtype=jnp.float32)
        adj = jax.random.uniform(k2, (N_NODES, N_NODES), dtype=jnp.float32)
        bound = 1.0 / np.sqrt(DIM)
        W = jax.random.uniform(k3, (DIM, DIM), minval=-bound, maxval=bound, dtype=jnp.float32)
        b = jax.random.uniform(k4, (DIM,), minval=-bound, maxval=bound, dtype=jnp.float32)
        return {'x': x, 'adj': adj, 'W': W, 'b': b}
    _L0_gnn_all = _L0_gnn_setup()
    _L0_gnn_in = {k: v for k, v in _L0_gnn_all.items() if k in ('W', 'b')}
    del _L0_gnn_all

    def _L1_gnn_setup():
        import jax, jax.numpy as jnp
        import numpy as np
        N = 4096
        D = 256
        key = jax.random.key(seed)
        ks = jax.random.split(key, 6)
        s = 1.0 / np.sqrt(D)
        return {'x': jax.random.normal(ks[0], (N, D), jnp.float32), 'spatial_encoding': jax.random.normal(ks[1], (N, N), jnp.float32), 'edge_encoding': jax.random.normal(ks[2], (N, N), jnp.float32), 'Wq': jax.random.normal(ks[3], (D, D), jnp.float32) * s, 'bq': jnp.zeros((D,), jnp.float32), 'Wk': jax.random.normal(ks[4], (D, D), jnp.float32) * s, 'bk': jnp.zeros((D,), jnp.float32), 'Wv': jax.random.normal(ks[5], (D, D), jnp.float32) * s, 'bv': jnp.zeros((D,), jnp.float32)}
    _L1_gnn_all = _L1_gnn_setup()
    _L1_gnn_in = {k: v for k, v in _L1_gnn_all.items() if k in ('Wq', 'bq', 'Wk', 'bk', 'Wv', 'bv')}
    del _L1_gnn_all
    return {'x': x, 'adj': adj, 'L0_gnn_W': _L0_gnn_in['W'], 'L0_gnn_b': _L0_gnn_in['b'], 'L1_gnn_Wq': _L1_gnn_in['Wq'], 'L1_gnn_bq': _L1_gnn_in['bq'], 'L1_gnn_Wk': _L1_gnn_in['Wk'], 'L1_gnn_bk': _L1_gnn_in['bk'], 'L1_gnn_Wv': _L1_gnn_in['Wv'], 'L1_gnn_bv': _L1_gnn_in['bv']}

def reference(x, adj, L0_gnn_W, L0_gnn_b, L1_gnn_Wq, L1_gnn_bq, L1_gnn_Wk, L1_gnn_bk, L1_gnn_Wv, L1_gnn_bv):
    import jax
    import jax.numpy as jnp

    def _L0_gnn_ref(x, adj, W, b):
        import jax, jax.numpy as jnp
        import numpy as np
        N_NODES = 4096
        DIM = 256
        agg = jnp.matmul(adj, x)
        out = jnp.matmul(agg, W.T) + b
        return jax.nn.relu(out)

    def _L1_gnn_ref(x, spatial_encoding, edge_encoding, Wq, bq, Wk, bk, Wv, bv):
        import jax, jax.numpy as jnp
        import numpy as np
        N = 4096
        D = 256
        q = x @ Wq.T + bq
        k = x @ Wk.T + bk
        v = x @ Wv.T + bv
        scale = 1.0 / jnp.sqrt(jnp.asarray(q.shape[-1], q.dtype))
        a = q @ k.T * scale + spatial_encoding + edge_encoding
        attn = jax.nn.softmax(a, axis=-1)
        return attn @ v
    x = _layernorm(x + _L0_gnn_ref(x, adj, L0_gnn_W, L0_gnn_b), axis=-1)
    x = _layernorm(x + _L1_gnn_ref(x, adj, adj, L1_gnn_Wq, L1_gnn_bq, L1_gnn_Wk, L1_gnn_bk, L1_gnn_Wv, L1_gnn_bv), axis=-1)
    return x

_drawn_inputs = setup_inputs


def setup_inputs(seed=0):
    import zlib

    import numpy as np

    out = dict(_drawn_inputs(seed))
    spreads = {'L1_gnn_bq': (0.0, 0.8), 'L1_gnn_bk': (0.0, 0.8), 'L1_gnn_bv': (0.0, 0.1)}
    factors = {}
    for name, (base, spread) in spreads.items():
        noise = np.random.default_rng([zlib.crc32(name.encode()), seed]).standard_normal(out[name].shape)
        drawn = base * np.exp(spread * noise) if base else spread * noise
        out[name] = jnp.asarray(drawn.astype(out[name].dtype))
    for name, factor in factors.items():
        out[name] = (out[name] * factor).astype(out[name].dtype)
    return out
```

```python
import concourse.bass as bass
from concourse import mybir
from contextlib import ExitStack

N, D, P = 4096, 256, 128
TILES = N // P
HALVES = D // P
BANK = 512
GROUPS = N // BANK
GT = BANK // P
AC = 4
ACW = N // AC
JA = ACW // P
SC = N // BANK
EPS = 1e-5
HI, LO = 0, 1
RSQRT_MAGIC = 0x5F3759DF
NEWTON_STEPS = 3

F32 = mybir.dt.float32
F32R = mybir.dt.float32r
I32 = mybir.dt.int32
ALU = mybir.AluOpType
ACT = mybir.ActivationFunctionType
AX_X = mybir.AxisListType.X


def two_layers(nc, xT, x, adjT, adj, w0T, wqT, wkT, wvT, b0, bq, bk, bv, eye, out):
    q_dram = nc.dram_tensor("q_scratch", (TILES, P, 2, HALVES, P), F32, kind="Internal").ap()
    x1_dram = nc.dram_tensor("x1_scratch", (TILES, P, D), F32, kind="Internal").ap()
    x1b_dram = nc.dram_tensor("x1_bv_scratch", (TILES, P, D), F32, kind="Internal").ap()

    base = (nc.sbuf_base + 63) // 64 * 64
    KB = 1024
    R_RHS, R_K, R_S, R_ADJ, R_SPLIT, R_Q, R_SMALL = (base + k * KB for k in (0, 64, 128, 160, 176, 192, 196))

    def at(name, shape, dt, offset):
        return nc.alloc_sbuf_tensor_at(name, shape, dt, offset=offset)

    rhs_split = at("rhs_split", [P, TILES, 2, D], F32R, R_RHS)
    a_split = at("a_split", [P, 2, AC, 2, ACW], F32R, R_K)
    k_split = at("k_split", [P, 2, HALVES, N], F32R, R_K)
    a_raw = at("a_raw", [P, AC, ACW], F32, R_S)
    x1_group = at("x1_group", [P, 2, GT, D], F32, R_S)
    q_stage = at("q_stage", [P, 2, 2, HALVES, BANK], F32R, R_S + 8 * KB)
    w_raw = at("w_raw", [P, 4, HALVES, D], F32, R_S + 24 * KB)
    scores = at("scores", [P, 2, N], F32, R_S)
    x0_raw = at("x0_raw", [P, 2, HALVES, BANK], F32, R_ADJ)
    w_split = at("w_split", [P, 3, 2, HALVES, D], F32R, R_ADJ)
    adj_ring = at("adj_ring", [P, AC, ACW], F32, R_ADJ)
    xT_split = at("xT_split", [P, 2, 2, HALVES, BANK], F32R, R_SPLIT)
    pT_split = at("pT_split", [P, 4, 2, GT, P], F32R, R_SPLIT)
    w0_split = at("w0_split", [P, 2, HALVES, D], F32R, R_Q)
    q_tile = at("q_tile", [P, 2, 2, HALVES, P], F32R, R_Q)

    small = [R_SMALL]

    def little(name, shape, dt=F32):
        words = 1
        for n in shape[1:]:
            words *= n
        t = at(name, shape, dt, small[0])
        small[0] += (4 * words + 31) // 32 * 32
        return t

    b0_all = little("b0_all", [P, D])
    bv_all = little("bv_all", [P, D])
    ident = little("ident", [P, P])
    resid = little("resid", [P, 2, D])
    acc = little("acc", [P, D])
    normed = little("normed", [P, 2, D])
    x1b = little("x1b", [P, 2, D])
    bq_raw = little("bq_raw", [P, HALVES])
    bq_col = little("bq_col", [P, HALVES])
    bk_col = little("bk_col", [P, HALVES])
    stats = little("stats", [P, 6])
    mean_var = little("mean_var", [P, 2])
    var_eps = little("var_eps", [P, 1])
    newton_a = little("newton_a", [P, 1])
    rstd = little("rstd", [P, 1])
    row_max8 = little("row_max8", [P, SC])
    row_max = little("row_max", [P, 1])
    neg_max = little("neg_max", [P, 2, 1])
    row_sum8 = little("row_sum8", [P, 2, SC])
    row_sum = little("row_sum", [P, 1])
    inv_sum = little("inv_sum", [P, 1])

    with ExitStack() as ctx:
        def psum(name):
            return ctx.enter_context(nc.psum_tensor(name, [P, BANK], F32))

        def sem(name):
            return ctx.enter_context(nc.semaphore(name))

        s_bank = [psum(f"s_bank{i}") for i in range(4)]
        t_bank = [psum(f"t_bank{i}") for i in range(2)]
        o_bank = [psum(f"o_bank{i}") for i in range(2)]

        w_loaded = sem("w_loaded")
        const_loaded = sem("const_loaded")
        w0_hi = sem("w0_hi")
        w0_ready = sem("w0_ready")
        wq_scaled = sem("wq_scaled")
        w_hi = sem("w_hi")
        w_ready = sem("w_ready")
        x0_loaded = [sem(f"x0_loaded{i}") for i in range(2)]
        x0_hi = sem("x0_hi")
        x0_split = sem("x0_split")
        y_product = sem("y_product")
        y_hi = sem("y_hi")
        y_ready = sem("y_ready")
        a_loaded = [sem(f"a_loaded{i}") for i in range(AC)]
        a_hi = sem("a_hi")
        a_ready = sem("a_ready")
        a_used = sem("a_used")
        agg_read = sem("agg_read")
        agg_biased = sem("agg_biased")
        x_loaded = [sem(f"x_loaded{i}") for i in range(2)]
        x_added = sem("x_added")
        x1_ready = sem("x1_ready")
        x1b_ready = sem("x1b_ready")
        x1_stored = [sem(f"x1_stored{i}") for i in range(2)]
        x1b_stored = [sem(f"x1b_stored{i}") for i in range(2)]
        g_loaded = [sem(f"g_loaded{i}") for i in range(2)]
        g_transposed = sem("g_transposed")
        g_hi = sem("g_hi")
        g_split = sem("g_split")
        g_used = sem("g_used")
        qkv_product = sem("qkv_product")
        qkv_hi = sem("qkv_hi")
        qkv_ready = sem("qkv_ready")
        q_stored = [sem(f"q_stored{i}") for i in range(2)]
        q_loaded = [sem(f"q_loaded{i}") for i in range(2)]
        adj_loaded = [sem(f"adj_loaded{i}") for i in range(AC)]
        x1b_loaded = [sem(f"x1b_loaded{i}") for i in range(2)]
        s_product = sem("s_product")
        s_ready = sem("s_ready")
        max_found = sem("max_found")
        max_ready = sem("max_ready")
        p_ready = sem("p_ready")
        p_transposed = sem("p_transposed")
        pT_hi = sem("pT_hi")
        pT_ready = sem("pT_ready")
        pv_done = sem("pv_done")
        sum_found = sem("sum_found")
        sum_inverted = sem("sum_inverted")
        o_half = sem("o_half")
        o_read = sem("o_read")
        out_ready = sem("out_ready")
        out_stored = [sem(f"out_stored{i}") for i in range(2)]
        ln_stats = sem("ln_stats")
        ln_mean = sem("ln_mean")
        ln_eps = sem("ln_eps")
        ln_shifted = sem("ln_shifted")
        ln_seed = sem("ln_seed")
        ln_newton = sem("ln_newton")

        held = {name: sem(f"held_{name}") for name in ("vector", "gpsimd")}

        def hold(engine, name, semaphore, value):
            engine.wait_ge(semaphore, value)
            engine.sem_inc(held[name], 1)

        block = ctx.enter_context(nc.Block())

        @block.sync
        def _(sp):
            sp.dma_start(w_raw[:, 0], w0T).then_inc(w_loaded, 16)

            def load_x0(i, slot, again):
                if again:
                    sp.wait_ge(x0_split, 2 * i + slot - 1)
                sp.dma_start(x0_raw[:, slot], xT[2 * i + slot]).then_inc(x0_loaded[slot], 16)

            load_x0(0, 0, False)
            load_x0(0, 1, False)
            for n, w in enumerate((wqT, wkT, wvT)):
                sp.dma_start(w_raw[:, n + 1], w).then_inc(w_loaded, 16)
            sp.dma_start(b0_all[:, :], b0.partition_broadcast(P)).then_inc(const_loaded, 16)
            sp.dma_start(bv_all[:, :], bv.partition_broadcast(P)).then_inc(const_loaded, 16)
            sp.dma_start(bq_raw[:, :], bq).then_inc(const_loaded, 16)
            sp.dma_start(bk_col[:, :], bk).then_inc(const_loaded, 16)
            sp.dma_start(ident[:, :], eye).then_inc(const_loaded, 16)
            for c in range(AC):
                sp.dma_start(a_raw[:, c], adjT[0][:, c]).then_inc(a_loaded[c], 16)
            for slot in range(2):
                sp.dma_start(resid[:, slot], x[slot]).then_inc(x_loaded[slot], 16)
            with sp.Fori(1, GROUPS // 2) as i:
                for slot in range(2):
                    load_x0(i, slot, True)

            def load_a(t):
                for c in range(AC):
                    sp.wait_ge(a_ready, AC * (t - 1) + c + 1)
                    sp.dma_start(a_raw[:, c], adjT[t][:, c]).then_inc(a_loaded[c], 16)

            load_a(1)
            with sp.Fori(1, TILES // 2) as i:
                for slot in range(2):
                    load_a(2 * i + slot)
                    sp.wait_ge(x_added, 2 * i + slot - 1)
                    sp.dma_start(resid[:, slot], x[2 * i + slot]).then_inc(x_loaded[slot], 16)

            sp.wait_ge(a_ready, AC * TILES)

            def load_group(i, slot, again):
                g = 2 * i + slot
                if again:
                    sp.wait_ge(g_transposed, HALVES * (g - 1))
                for s in range(2):
                    sp.wait_ge(x1_stored[s], 16 * GT // 2 * (g + 1))
                sp.dma_start(x1_group[:, slot], x1_dram[bass.ds(GT * g, GT)].rearrange("i p d -> p i d")
                             ).then_inc(g_loaded[slot], 16)

            load_group(0, 0, False)
            load_group(0, 1, False)
            with sp.Fori(1, GROUPS // 2) as i:
                for slot in range(2):
                    load_group(i, slot, True)

            sp.wait_ge(x_added, TILES)
            for s in range(2):
                sp.wait_ge(x1b_stored[s], 16 * TILES // 2)
                sp.wait_ge(q_stored[s], 16 * GT * GROUPS // 2)
            for slot in range(2):
                sp.dma_start(q_tile[:, slot].bitcast(F32), q_dram[slot]).then_inc(q_loaded[slot], 16)
            sp.wait_ge(qkv_product, 6 * GROUPS)
            for c in range(AC):
                sp.dma_start(adj_ring[:, c], adj[0][:, bass.ds(c * ACW, ACW)]).then_inc(adj_loaded[c], 16)
            for slot in range(2):
                sp.dma_start(resid[:, slot], x1b_dram[slot]).then_inc(x1b_loaded[slot], 16)

            def load_adj(t):
                for c in range(AC):
                    sp.wait_ge(s_ready, SC * (t - 1) + SC // AC * (c + 1))
                    sp.dma_start(adj_ring[:, c], adj[t][:, bass.ds(c * ACW, ACW)]).then_inc(adj_loaded[c], 16)

            load_adj(1)
            with sp.Fori(1, TILES // 2) as i:
                for slot in range(2):
                    t = 2 * i + slot
                    sp.wait_ge(s_product, SC * (t - 1))
                    sp.dma_start(q_tile[:, slot].bitcast(F32), q_dram[t]).then_inc(q_loaded[slot], 16)
                    load_adj(t)
                    sp.wait_ge(o_read, t - 1)
                    sp.dma_start(resid[:, slot], x1b_dram[t]).then_inc(x1b_loaded[slot], 16)

        @block.tensor
        def _(pe):
            def three_passes(bank, left, right, first, last):
                pe.matmul(bank, left(HI), right(HI), start=first, stop=False)
                pe.matmul(bank, left(HI), right(LO), start=False, stop=False)
                return pe.matmul(bank, left(LO), right(HI), start=False, stop=last)

            def project_rows(bank, slot, pair, w):
                for k in range(2):
                    rows = slice((2 * pair + k) * P, (2 * pair + k + 1) * P)
                    for h in range(HALVES):
                        done = three_passes(bank[:, k * D:(k + 1) * D],
                                            lambda part: xT_split[:, slot, part, h, rows],
                                            lambda part: w(part, h),
                                            h == 0, h == HALVES - 1)
                return done

            pe.wait_ge(w0_ready, 1)

            def y_group(i, slot, again):
                g = 2 * i + slot
                pe.wait_ge(x0_split, g + 1)
                for pair in range(2):
                    bank = s_bank[2 * slot + pair]
                    if again:
                        pe.wait_ge(y_ready, 2 * (g - 2) + pair + 1)
                    project_rows(bank, slot, pair, lambda part, h: w0_split[:, part, h, :]).then_inc(y_product, 1)

            y_group(0, 0, False)
            y_group(0, 1, False)
            with pe.Fori(1, GROUPS // 2) as i:
                y_group(i, 0, True)
                y_group(i, 1, True)

            pe.wait_ge(y_ready, 2 * GROUPS)

            def aggregate(t, slot, again):
                if again:
                    pe.wait_ge(agg_read, t - 1)
                for c in range(AC):
                    pe.wait_ge(a_ready, AC * t + c + 1)
                    for j in range(JA):
                        jt = c * JA + j
                        cols = slice(j * P, (j + 1) * P)
                        pe.matmul(o_bank[slot][:, :], a_split[:, slot, c, HI, cols], rhs_split[:, jt, :, :],
                                  start=(jt == 0), stop=False)
                        done = pe.matmul(o_bank[slot][:, D:2 * D], a_split[:, slot, c, LO, cols],
                                         rhs_split[:, jt, HI, :], start=False, stop=(jt == TILES - 1))
                    done.then_inc(a_used, 1)

            aggregate(0, 0, False)
            aggregate(1, 1, False)
            with pe.Fori(1, TILES // 2) as i:
                aggregate(2 * i, 0, True)
                aggregate(2 * i + 1, 1, True)

            result_bank = s_bank + o_bank
            pe.wait_ge(const_loaded, 80)
            pe.wait_ge(w_ready, 3)
            pe.wait_ge(agg_read, TILES)

            def transpose_group(i, slot, again):
                g = 2 * i + slot
                pe.wait_ge(g_loaded[slot], 16 * (i + 1))
                for h in range(HALVES):
                    if again:
                        pe.wait_ge(g_split, HALVES * (g - 1) + h + 1)
                    for k in range(GT):
                        done = pe.transpose(t_bank[h][:, k * P:(k + 1) * P],
                                            x1_group[:, slot, k, h * P:(h + 1) * P], ident[:, :])
                    done.then_inc(g_transposed, 1)

            def project_columns(i, slot, which, again):
                g = 2 * i + slot
                for half in range(HALVES):
                    r = 2 * which + half
                    if again:
                        pe.wait_ge(qkv_ready, 6 * (g - 1) + r + 1)
                    feats = slice(half * P, (half + 1) * P)
                    for h in range(HALVES):
                        done = three_passes(result_bank[r][:, :],
                                            lambda part: w_split[:, which, part, h, feats],
                                            lambda part: xT_split[:, slot, part, h, :],
                                            h == 0, h == HALVES - 1)
                    done.then_inc(qkv_product, 1)

            def project_v(i, slot, again):
                g = 2 * i + slot
                for pair in range(2):
                    r = 4 + pair
                    if again:
                        pe.wait_ge(qkv_ready, 6 * (g - 1) + r + 1)
                    project_rows(result_bank[r], slot, pair,
                                 lambda part, h: w_split[:, 2, part, h, :]).then_inc(qkv_product, 1)

            def qkv_group(i, slot, again, last):
                g = 2 * i + slot
                pe.wait_ge(g_split, HALVES * (g + 1))
                project_columns(i, slot, 0, again)
                project_columns(i, slot, 1, again)
                if not last:
                    transpose_group(i + slot, 1 - slot, True)
                project_v(i, slot, again)

            transpose_group(0, 0, False)
            qkv_group(0, 0, False, False)
            qkv_group(0, 1, True, False)
            with pe.Fori(1, GROUPS // 2 - 1) as i:
                qkv_group(i, 0, True, False)
                qkv_group(i, 1, True, False)
            qkv_group(GROUPS // 2 - 1, 0, True, False)
            qkv_group(GROUPS // 2 - 1, 1, True, True)

            pe.wait_ge(qkv_ready, 6 * GROUPS)

            def score(i, slot, c, again):
                t = 2 * i + slot
                if c == 0:
                    pe.wait_ge(q_loaded[slot], 16 * (i + 1))
                if again or c >= 4:
                    pe.wait_ge(s_ready, SC * t + c - 3)
                cols = slice(c * BANK, (c + 1) * BANK)
                for h in range(HALVES):
                    done = three_passes(s_bank[c % 4][:, :],
                                        lambda part: q_tile[:, slot, part, h, :],
                                        lambda part: k_split[:, part, h, cols],
                                        h == 0, h == HALVES - 1)
                done.then_inc(s_product, 1)

            def transpose_p(t, slot, c, again):
                pe.wait_ge(p_ready, SC * t + c + 1)
                if again or c >= 2:
                    pe.wait_ge(pT_ready, SC * t + c - 1)
                for k in range(GT):
                    lo = c * BANK + k * P
                    done = pe.transpose(t_bank[c % 2][:, k * P:(k + 1) * P], scores[:, slot, lo:lo + P], ident[:, :])
                done.then_inc(p_transposed, 1)

            def attend(t, slot, c, again):
                if c == 0 and again:
                    pe.wait_ge(o_read, t - 1)
                pe.wait_ge(pT_ready, SC * t + c + 1)
                for k in range(GT):
                    jt = c * GT + k
                    pe.matmul(o_bank[slot][:, :], pT_split[:, c % 4, HI, k, :], rhs_split[:, jt, :, :],
                              start=(jt == 0), stop=False)
                    done = pe.matmul(o_bank[slot][:, D:2 * D], pT_split[:, c % 4, LO, k, :],
                                     rhs_split[:, jt, HI, :], start=False, stop=(jt == TILES - 1))
                done.then_inc(pv_done, 1)

            def step(i, slot, before, last):
                t = 2 * i + slot
                ahead = (i + slot, 1 - slot)
                for c in range(SC + 2):
                    if c < SC and not last:
                        score(*ahead, c, True)
                    if 1 <= c <= SC:
                        transpose_p(t, slot, c - 1, before >= 1)
                    if c >= 2:
                        attend(t, slot, c - 2, before >= 2)

            for c in range(SC):
                score(0, 0, c, False)
            step(0, 0, 0, False)
            step(0, 1, 1, False)
            with pe.Fori(1, TILES // 2 - 1) as i:
                step(i, 0, 2, False)
                step(i, 1, 2, False)
            step(TILES // 2 - 1, 0, 2, False)
            step(TILES // 2 - 1, 1, 2, True)

        @block.scalar
        def _(act):
            act.wait_ge(w_loaded, 64)
            act.activation(w0_split[:, HI], w_raw[:, 0], ACT.Copy).then_inc(w0_hi, 1)

            def y_group(i, slot, again):
                g = 2 * i + slot
                act.wait_ge(x0_loaded[slot], 16 * (i + 1))
                if again:
                    act.wait_ge(y_product, 2 * (g - 1))
                act.activation(xT_split[:, slot, HI], x0_raw[:, slot], ACT.Copy).then_inc(x0_hi, 1)

            def y_rows(i, slot):
                for pair in range(2):
                    act.wait_ge(y_product, 2 * (2 * i + slot) + pair + 1)
                    act.activation(rhs_split[:, bass.ds(GT * (2 * i + slot) + 2 * pair, 2), HI, :],
                                   s_bank[2 * slot + pair][:, :].rearrange("p (k d) -> p k d", k=2),
                                   ACT.Copy).then_inc(y_hi, 1)

            y_group(0, 0, False)
            y_group(0, 1, False)
            with act.Fori(1, GROUPS // 2) as i:
                y_rows(i - 1, 0)
                y_group(i, 0, True)
                y_rows(i - 1, 1)
                y_group(i, 1, True)
            y_rows(GROUPS // 2 - 1, 0)
            y_rows(GROUPS // 2 - 1, 1)

            def a_tile(i, slot, again):
                t = 2 * i + slot
                for c in range(AC):
                    act.wait_ge(a_loaded[c], 16 * (t + 1))
                    if again:
                        act.wait_ge(a_used, AC * (t - 2) + c + 1)
                    act.activation(a_split[:, slot, c, HI], a_raw[:, c], ACT.Copy).then_inc(a_hi, 1)

            a_tile(0, 0, False)
            a_tile(0, 1, False)
            act.wait_ge(wq_scaled, 1)
            for n in range(3):
                act.activation(w_split[:, n, HI], w_raw[:, n + 1], ACT.Copy).then_inc(w_hi, 1)
            with act.Fori(1, TILES // 2) as i:
                a_tile(i, 0, True)
                a_tile(i, 1, True)

            result_bank = s_bank + o_bank

            def group_hi(i, slot, again):
                g = 2 * i + slot
                for h in range(HALVES):
                    act.wait_ge(g_transposed, HALVES * g + h + 1)
                    if again:
                        act.wait_ge(qkv_product, 6 * (g - 1))
                    act.activation(xT_split[:, slot, HI, h], t_bank[h][:, :], ACT.Copy).then_inc(g_hi, 1)

            def result_hi(i, slot, r, again):
                g = 2 * i + slot
                act.wait_ge(qkv_product, 6 * g + r + 1)
                if r < 2:
                    if again:
                        act.wait_ge(q_stored[slot], 16 * GT * i)
                    act.activation(q_stage[:, slot, HI, r], result_bank[r][:, :], ACT.Identity,
                                   bias=bq_col[:, r:r + 1]).then_inc(qkv_hi, 1)
                elif r < 4:
                    act.activation(k_split[:, HI, r - 2, bass.ds(g * BANK, BANK)], result_bank[r][:, :],
                                   ACT.Identity, bias=bk_col[:, r - 2:r - 1]).then_inc(qkv_hi, 1)
                else:
                    act.activation(rhs_split[:, bass.ds(GT * g + 2 * (r - 4), 2), HI, :],
                                   result_bank[r][:, :].rearrange("p (k d) -> p k d", k=2),
                                   ACT.Copy).then_inc(qkv_hi, 1)

            def qkv_group(i, slot, again, last):
                for r in range(4):
                    result_hi(i, slot, r, again)
                if not last:
                    group_hi(i + slot, 1 - slot, again or slot == 1)
                for r in (4, 5):
                    result_hi(i, slot, r, again)

            group_hi(0, 0, False)
            qkv_group(0, 0, False, False)
            qkv_group(0, 1, False, False)
            with act.Fori(1, GROUPS // 2 - 1) as i:
                qkv_group(i, 0, True, False)
                qkv_group(i, 1, True, False)
            qkv_group(GROUPS // 2 - 1, 0, True, False)
            qkv_group(GROUPS // 2 - 1, 1, True, True)

            def step(i, slot, first):
                t = 2 * i + slot
                for c in range(SC + 1):
                    if c < SC:
                        if c == 0:
                            act.wait_ge(max_ready, t + 1)
                        s = scores[:, slot, c * BANK:(c + 1) * BANK]
                        act.activation(s, s, ACT.Exp, bias=neg_max[:, slot, :], scale=2.0,
                                       accum_out=row_sum8[:, slot, c:c + 1]).then_inc(p_ready, 1)
                    if c >= 1:
                        k = c - 1
                        act.wait_ge(p_transposed, SC * t + k + 1)
                        if not (first and k < 4):
                            act.wait_ge(pv_done, SC * t + k - 3)
                        act.activation(pT_split[:, k % 4, HI].rearrange("p k n -> p (k n)"),
                                       t_bank[k % 2][:, :], ACT.Copy).then_inc(pT_hi, 1)

            step(0, 0, True)
            step(0, 1, False)
            with act.Fori(1, TILES // 2) as i:
                step(i, 0, False)
                step(i, 1, False)

        @block.vector
        def _(dve):
            def layer_norm(n, write):
                dve.bn_stats(stats[:, :], acc[:, :]).then_inc(ln_stats, 1)
                hold(dve, "vector", ln_stats, n + 1)
                dve.bn_aggr(mean_var[:, :], stats[:, :]).then_inc(ln_mean, 1)
                dve.wait_ge(ln_mean, n + 1)
                dve.tensor_scalar(var_eps[:, :], mean_var[:, 1:2], EPS, None, ALU.add).then_inc(ln_eps, 1)
                dve.wait_ge(ln_eps, n + 1)
                dve.tensor_scalar(newton_a[:, :].bitcast(I32), var_eps[:, :].bitcast(I32), 1, None,
                                  ALU.logical_shift_right).then_inc(ln_shifted, 1)
                dve.wait_ge(ln_shifted, n + 1)
                dve.tensor_scalar(rstd[:, :].bitcast(I32), newton_a[:, :].bitcast(I32), -1.0,
                                  float(RSQRT_MAGIC), ALU.mult, ALU.add).then_inc(ln_seed, 1)
                dve.wait_ge(ln_seed, n + 1)
                for k in range(NEWTON_STEPS):
                    before = 3 * NEWTON_STEPS * n + 3 * k
                    dve.scalar_tensor_tensor(out=newton_a[:, :], in0=rstd[:, :], scalar=rstd[:, :],
                                             in1=var_eps[:, :], op0=ALU.mult, op1=ALU.mult).then_inc(ln_newton, 1)
                    dve.wait_ge(ln_newton, before + 1)
                    dve.tensor_scalar(newton_a[:, :], newton_a[:, :], -0.5, 1.5, ALU.mult, ALU.add).then_inc(ln_newton, 1)
                    dve.wait_ge(ln_newton, before + 2)
                    dve.tensor_tensor(rstd[:, :], rstd[:, :], newton_a[:, :], ALU.mult).then_inc(ln_newton, 1)
                    dve.wait_ge(ln_newton, before + 3)
                return dve.tensor_scalar(write, acc[:, :], mean_var[:, 0:1], rstd[:, :], ALU.subtract, ALU.mult)

            def lo_part(out, whole, hi):
                return dve.tensor_tensor(out, whole, hi.bitcast(F32), ALU.subtract)

            dve.wait_ge(w0_hi, 1)
            lo_part(w0_split[:, LO], w_raw[:, 0], w0_split[:, HI]).then_inc(w0_ready, 1)

            def y_group(i, slot):
                dve.wait_ge(x0_hi, 2 * i + slot + 1)
                lo_part(xT_split[:, slot, LO], x0_raw[:, slot], xT_split[:, slot, HI]).then_inc(x0_split, 1)

            def y_rows(i, slot):
                for pair in range(2):
                    dve.wait_ge(y_hi, 2 * (2 * i + slot) + pair + 1)
                    rows = bass.ds(GT * (2 * i + slot) + 2 * pair, 2)
                    lo_part(rhs_split[:, rows, LO, :],
                            s_bank[2 * slot + pair][:, :].rearrange("p (k d) -> p k d", k=2),
                            rhs_split[:, rows, HI, :]).then_inc(y_ready, 1)

            y_group(0, 0)
            y_group(0, 1)
            with dve.Fori(1, GROUPS // 2) as i:
                y_rows(i - 1, 0)
                y_group(i, 0)
                y_rows(i - 1, 1)
                y_group(i, 1)
            y_rows(GROUPS // 2 - 1, 0)
            y_rows(GROUPS // 2 - 1, 1)

            scale = 0.5 * D ** -0.5
            dve.wait_ge(const_loaded, 80)
            dve.tensor_scalar(bq_col[:, :], bq_raw[:, :], scale, None, ALU.mult)
            dve.tensor_scalar(w_raw[:, 1], w_raw[:, 1], scale, None, ALU.mult).then_inc(wq_scaled, 1)

            def a_tile(t, slot):
                for c in range(AC):
                    dve.wait_ge(a_hi, AC * t + c + 1)
                    lo_part(a_split[:, slot, c, LO], a_raw[:, c], a_split[:, slot, c, HI]).then_inc(a_ready, 1)

            def first_layer(i, slot, again):
                t = 2 * i + slot
                if again or slot == 1:
                    dve.wait_ge(x1_ready, t)
                dve.wait_ge(a_used, AC * (t + 1))
                dve.tensor_tensor(acc[:, :], o_bank[slot][:, D:2 * D], b0_all[:, :], ALU.add).then_inc(agg_biased, 1)
                dve.wait_ge(agg_biased, t + 1)
                dve.tensor_tensor(acc[:, :], o_bank[slot][:, 0:D], acc[:, :], ALU.add).then_inc(agg_read, 1)
                dve.wait_ge(agg_read, t + 1)
                dve.wait_ge(x_loaded[slot], 16 * (i + 1))
                dve.scalar_tensor_tensor(out=acc[:, :], in0=acc[:, :], scalar=0.0, in1=resid[:, slot, :],
                                         op0=ALU.max, op1=ALU.add).then_inc(x_added, 1)
                dve.wait_ge(x_added, t + 1)
                if again:
                    dve.wait_ge(x1_stored[slot], 16 * i)
                    dve.wait_ge(x1b_ready, t - 1)
                layer_norm(t, normed[:, slot, :]).then_inc(x1_ready, 1)

            a_tile(0, 0)
            a_tile(1, 1)
            for n in range(3):
                dve.wait_ge(w_hi, n + 1)
                lo_part(w_split[:, n, LO], w_raw[:, n + 1], w_split[:, n, HI]).then_inc(w_ready, 1)
            first_layer(0, 0, False)
            a_tile(2, 0)
            first_layer(0, 1, False)
            a_tile(3, 1)
            with dve.Fori(1, TILES // 2 - 1) as i:
                first_layer(i, 0, True)
                a_tile(2 * i + 2, 0)
                first_layer(i, 1, True)
                a_tile(2 * i + 3, 1)
            first_layer(TILES // 2 - 1, 0, True)
            first_layer(TILES // 2 - 1, 1, True)

            result_bank = s_bank + o_bank

            def group_lo(i, slot):
                g = 2 * i + slot
                for h in range(HALVES):
                    dve.wait_ge(g_hi, HALVES * g + h + 1)
                    lo_part(xT_split[:, slot, LO, h], t_bank[h][:, :], xT_split[:, slot, HI, h]).then_inc(g_split, 1)

            def result_lo(i, slot, r):
                g = 2 * i + slot
                dve.wait_ge(qkv_hi, 6 * g + r + 1)
                if r < 4:
                    hi, lo, bias = (
                        (q_stage[:, slot, HI, r], q_stage[:, slot, LO, r], bq_col[:, r:r + 1]) if r < 2 else
                        (k_split[:, HI, r - 2, bass.ds(g * BANK, BANK)],
                         k_split[:, LO, r - 2, bass.ds(g * BANK, BANK)], bk_col[:, r - 2:r - 1]))
                    dve.scalar_tensor_tensor(out=lo, in0=result_bank[r][:, :], scalar=bias, in1=hi.bitcast(F32),
                                             op0=ALU.add, op1=ALU.subtract).then_inc(qkv_ready, 1)
                else:
                    rows = bass.ds(GT * g + 2 * (r - 4), 2)
                    lo_part(rhs_split[:, rows, LO, :], result_bank[r][:, :].rearrange("p (k d) -> p k d", k=2),
                            rhs_split[:, rows, HI, :]).then_inc(qkv_ready, 1)

            def qkv_group(i, slot, last):
                for r in range(4):
                    result_lo(i, slot, r)
                if not last:
                    group_lo(i + slot, 1 - slot)
                for r in (4, 5):
                    result_lo(i, slot, r)

            group_lo(0, 0)
            with dve.Fori(0, GROUPS // 2 - 1) as i:
                qkv_group(i, 0, False)
                qkv_group(i, 1, False)
            qkv_group(GROUPS // 2 - 1, 0, False)
            qkv_group(GROUPS // 2 - 1, 1, True)

            def add_adj(t, slot, c, again):
                if c % 2 == 0:
                    dve.wait_ge(adj_loaded[c // 2], 16 * (t + 1))
                if c == 0 and again:
                    dve.wait_ge(p_transposed, SC * (t - 1))
                hold(dve, "vector", s_product, SC * t + c + 1)
                cols = slice(c * BANK, (c + 1) * BANK)
                dve.tensor_tensor_reduce(out=scores[:, slot, cols], in0=s_bank[c % 4][:, :],
                                         in1=adj_ring[:, c // 2, (c % 2) * BANK:(c % 2 + 1) * BANK],
                                         scale=1.0, scalar=-3.0e38, op0=ALU.add, op1=ALU.max,
                                         accum_out=row_max8[:, c:c + 1]).then_inc(s_ready, 1)

            def whole_max(t, slot):
                dve.wait_ge(s_ready, SC * (t + 1))
                dve.tensor_reduce(row_max[:, :], row_max8[:, :], AX_X, ALU.max).then_inc(max_found, 1)
                dve.wait_ge(max_found, t + 1)
                dve.tensor_scalar(neg_max[:, slot, :], row_max[:, :], -2.0, None, ALU.mult).then_inc(max_ready, 1)

            def pT_lo(t, c):
                dve.wait_ge(pT_hi, SC * t + c + 1)
                hi, lo = (pT_split[:, c % 4, part].rearrange("p k n -> p (k n)") for part in (HI, LO))
                lo_part(lo, t_bank[c % 2][:, :], hi).then_inc(pT_ready, 1)

            def residual(i, slot, again):
                t = 2 * i + slot
                if again:
                    dve.wait_ge(out_ready, t)
                dve.tensor_reduce(row_sum[:, :], row_sum8[:, slot, :], AX_X, ALU.add).then_inc(sum_found, 1)
                dve.wait_ge(sum_found, t + 1)
                dve.reciprocal(inv_sum[:, :], row_sum[:, :]).then_inc(sum_inverted, 1)
                dve.wait_ge(sum_inverted, t + 1)
                dve.wait_ge(pv_done, SC * (t + 1))
                dve.wait_ge(x1b_loaded[slot], 16 * (i + 1))
                dve.scalar_tensor_tensor(out=acc[:, :], in0=o_bank[slot][:, D:2 * D], scalar=inv_sum[:, :],
                                         in1=resid[:, slot, :], op0=ALU.mult, op1=ALU.add).then_inc(o_half, 1)
                dve.wait_ge(o_half, t + 1)
                dve.scalar_tensor_tensor(out=acc[:, :], in0=o_bank[slot][:, 0:D], scalar=inv_sum[:, :],
                                         in1=acc[:, :], op0=ALU.mult, op1=ALU.add).then_inc(o_read, 1)
                dve.wait_ge(o_read, t + 1)

            def second_norm(i, slot, again):
                if again:
                    dve.wait_ge(out_stored[slot], 16 * i)
                layer_norm(TILES + 2 * i + slot, normed[:, slot, :]).then_inc(out_ready, 1)

            def step(i, slot, before, last):
                t = 2 * i + slot
                behind = (i - 1 + slot, 1 - slot)
                for c in range(SC + 1):
                    if c < SC and not last:
                        add_adj(t + 1, 1 - slot, c, before >= 1)
                        if c == SC - 1:
                            whole_max(t + 1, 1 - slot)
                    if c >= 1:
                        pT_lo(t, c - 1)
                    if c == 2 and before >= 1:
                        residual(*behind, before >= 2)
                    if c == 4 and before >= 1:
                        second_norm(*behind, before >= 3)

            for c in range(SC):
                add_adj(0, 0, c, False)
            whole_max(0, 0)
            step(0, 0, 0, False)
            for slot in range(2):
                dve.wait_ge(x1_stored[slot], 16 * TILES // 2)
            dve.wait_ge(x1b_ready, TILES)
            dve.wait_ge(x1_ready, TILES)
            step(0, 1, 1, False)
            step(1, 0, 2, False)
            step(1, 1, 3, False)
            with dve.Fori(2, TILES // 2 - 1) as i:
                step(i, 0, 3, False)
                step(i, 1, 3, False)
            step(TILES // 2 - 1, 0, 3, False)
            step(TILES // 2 - 1, 1, 3, True)
            residual(TILES // 2 - 1, 1, True)
            second_norm(TILES // 2 - 1, 1, True)

        @block.gpsimd
        def _(pool):
            pool.wait_ge(const_loaded, 80)

            def keep_x1(i, slot, again):
                t = 2 * i + slot
                pool.wait_ge(x1_ready, t + 1)
                if again:
                    pool.wait_ge(x1b_stored[slot], 16 * i)
                pool.tensor_tensor(x1b[:, slot, :], normed[:, slot, :], bv_all[:, :], ALU.add).then_inc(x1b_ready, 1)
                pool.dma_start(x1_dram[t], normed[:, slot, :]).then_inc(x1_stored[slot], 16)
                hold(pool, "gpsimd", x1b_ready, t + 1)
                pool.dma_start(x1b_dram[t], x1b[:, slot, :]).then_inc(x1b_stored[slot], 16)

            keep_x1(0, 0, False)
            keep_x1(0, 1, False)
            with pool.Fori(1, TILES // 2) as i:
                keep_x1(i, 0, True)
                keep_x1(i, 1, True)

            with pool.Fori(0, GROUPS // 2) as i:
                for slot in range(2):
                    g = 2 * i + slot
                    hold(pool, "gpsimd", qkv_ready, 6 * g + HALVES)
                    for k in range(GT):
                        pool.dma_start(q_dram[GT * g + k].rearrange("p s h n -> p (s h) n"),
                                       q_stage[:, slot].bitcast(F32).rearrange("p s h n -> p (s h) n")[:, :, k * P:(k + 1) * P]
                                       ).then_inc(q_stored[slot], 16)

            with pool.Fori(0, TILES // 2) as i:
                for slot in range(2):
                    t = 2 * i + slot
                    hold(pool, "gpsimd", out_ready, t + 1)
                    pool.dma_start(out[t], normed[:, slot, :]).then_inc(out_stored[slot], 16)
            for slot in range(2):
                pool.wait_ge(out_stored[slot], 16 * TILES // 2)


def kernel(x, adj, L0_gnn_W, L0_gnn_b, L1_gnn_Wq, L1_gnn_bq, L1_gnn_Wk, L1_gnn_bk, L1_gnn_Wv, L1_gnn_bv):
    import numpy as np
    import concourse.bacc as bacc
    from concourse.bass_utils import run_bass_kernel_spmd

    x, adj = np.asarray(x), np.asarray(adj)

    def features_first(w):
        return np.ascontiguousarray(np.asarray(w).T.reshape(HALVES, P, D).transpose(1, 0, 2))

    def column(b):
        return np.ascontiguousarray(np.asarray(b).reshape(HALVES, P).T)

    arrays = {
        "xT": np.ascontiguousarray(x.reshape(GROUPS, BANK, HALVES, P).transpose(0, 3, 2, 1)),
        "x": np.ascontiguousarray(x.reshape(TILES, P, D)),
        "adjT": np.ascontiguousarray(
            adj.reshape(TILES, P, AC, JA, P).transpose(0, 4, 2, 3, 1)).reshape(TILES, P, AC, ACW),
        "adj": np.ascontiguousarray(adj.reshape(TILES, P, N)),
        "w0T": features_first(L0_gnn_W),
        "wqT": features_first(L1_gnn_Wq),
        "wkT": features_first(L1_gnn_Wk),
        "wvT": features_first(L1_gnn_Wv),
        "b0": np.ascontiguousarray(L0_gnn_b),
        "bq": column(L1_gnn_bq),
        "bk": column(L1_gnn_bk),
        "bv": np.ascontiguousarray(L1_gnn_bv),
        "eye": np.eye(P, dtype=np.float32),
    }
    nc = bacc.Bacc("TRN2", target_bir_lowering=False, num_devices=1)
    args = [nc.dram_tensor(f"in_{name}", a.shape, mybir.dt.from_np(a.dtype), kind="ExternalInput").ap()
            for name, a in arrays.items()]
    out = nc.dram_tensor("out", (TILES, P, D), F32, kind="ExternalOutput").ap()
    two_layers(nc, *args, out)
    r = run_bass_kernel_spmd(nc, [{f"in_{name}": a for name, a in arrays.items()}], core_ids=[0])
    return r.results[0]["out"].reshape(N, D)
```

```python
import concourse.bass as bass
from concourse import mybir
from contextlib import ExitStack

N, D, P = 4096, 256, 128
TILES = N // P
HALVES = D // P
BANK = 512
GROUPS = N // BANK
GT = BANK // P
AC = 4
ACW = N // AC
JA = ACW // P
SC = 4
SCW = N // SC
HC = N // BANK
S = 32
QUADS = P // S
QW = N // QUADS
PC = 4
CT = TILES // PC
EPS = 1e-5
HI, LO = 0, 1
RSQRT_MAGIC = 0x5F3759DF
NEWTON_STEPS = 3

F32 = mybir.dt.float32
F32R = mybir.dt.float32r
I32 = mybir.dt.int32
ALU = mybir.AluOpType
ACT = mybir.ActivationFunctionType
AX_X = mybir.AxisListType.X


def two_layers(nc, xT, x, adjT, adj, w0T, wqT, wkT, wvT, b0, bq, bk, bv, eye, reorder, out):
    q_dram = nc.dram_tensor("q_scratch", (TILES, P, 2, HALVES, P), F32, kind="Internal").ap()
    x1_dram = nc.dram_tensor("x1_scratch", (TILES, P, D), F32, kind="Internal").ap()
    x1b_dram = nc.dram_tensor("x1_bv_scratch", (TILES, P, D), F32, kind="Internal").ap()

    base = (nc.sbuf_base + 63) // 64 * 64
    KB = 1024
    R_RHS, R_K, R_SPLIT, R_Q, R_WORK, R_SMALL = (base + k * KB for k in (0, 64, 128, 144, 148, 200))

    def at(name, shape, dt, offset):
        return nc.alloc_sbuf_tensor_at(name, shape, dt, offset=offset)

    rhs_split = at("rhs_split", [P, TILES, 2, D], F32R, R_RHS)
    a_split = at("a_split", [P, 2, AC, 2, ACW], F32R, R_K)
    k_split = at("k_split", [P, 2, HALVES, N], F32R, R_K)
    xT_split = at("xT_split", [P, 2, 2, HALVES, BANK], F32R, R_SPLIT)
    pT_split = at("pT_split", [P, 4, 2, GT, P], F32R, R_SPLIT)
    w0_split = at("w0_split", [P, 2, HALVES, D], F32R, R_Q)
    q_tile = at("q_tile", [P, 2, 2, HALVES, P], F32R, R_Q)
    a_raw = at("a_raw", [P, AC, ACW], F32, R_WORK)
    w_raw = at("w_raw", [P, 4, HALVES, D], F32, R_WORK + 16 * KB)
    x0_raw = at("x0_raw", [P, 2, HALVES, BANK], F32, R_WORK + 24 * KB)
    x1_group = at("x1_group", [P, 2, GT, D], F32, R_WORK)
    q_stage = at("q_stage", [P, 2, 2, HALVES, BANK], F32R, R_WORK + 8 * KB)
    w_split = at("w_split", [P, 3, 2, HALVES, D], F32R, R_WORK + 24 * KB)
    q_raw = at("q_raw", [P, HALVES, BANK], F32, R_WORK + 48 * KB)
    b0_all = at("b0_all", [P, D], F32, R_WORK + 36 * KB)
    bv_all = at("bv_all", [P, D], F32, R_WORK + 37 * KB)
    x1b = at("x1b", [P, 2, D], F32, R_WORK + 38 * KB)
    scores = at("scores", [P, N], F32, R_WORK)
    dealt = at("dealt", [P, QUADS, QW], F32, R_WORK + 16 * KB)
    pT = at("pT", [P, 2, CT, P], F32, R_WORK + 32 * KB)
    adj_ring = at("adj_ring", [P, SC - 1, SCW], F32, R_WORK + 40 * KB)

    small = [R_SMALL]

    def little(name, shape, dt=F32):
        words = 1
        for n in shape[1:]:
            words *= n
        t = at(name, shape, dt, small[0])
        small[0] += (4 * words + 31) // 32 * 32
        return t

    ident = little("ident", [P, P])
    to_tile = little("to_tile", [P, P])
    resid = little("resid", [P, 2, D])
    acc = little("acc", [P, 2, D])
    normed = little("normed", [P, 2, D])
    bq_raw = little("bq_raw", [P, HALVES])
    bq_col = little("bq_col", [P, HALVES])
    bk_col = little("bk_col", [P, HALVES])
    stats = little("stats", [P, 6])
    mean_var = little("mean_var", [P, 2, 2])
    var_eps = little("var_eps", [P, 2, 1])
    half_bits = little("half_bits", [P, 1])
    guess = little("guess", [P, 2, 1])
    newton_a = little("newton_a", [P, 1])
    rstd = little("rstd", [P, 1])
    row_max_of = little("row_max_of", [P, SC])
    row_max = little("row_max", [P, 1])
    neg_max = little("neg_max", [P, 2, 1])
    row_sum_of = little("row_sum_of", [P, 2, SC])
    row_sum = little("row_sum", [P, 1])
    inv_sum = little("inv_sum", [P, 2, 1])

    with ExitStack() as ctx:
        def psum(name):
            return ctx.enter_context(nc.psum_tensor(name, [P, BANK], F32))

        def sem(name):
            return ctx.enter_context(nc.semaphore(name))

        s_pair = [ctx.enter_context(nc.psum_tensor(f"s_pair{i}", [P, 2, BANK], F32)) for i in range(2)]
        s_bank = [s_pair[i // 2][:, i % 2, :] for i in range(4)]
        t_bank = [psum(f"t_bank{i}") for i in range(2)]
        o_bank = [psum(f"o_bank{i}") for i in range(2)]

        w0_loaded = sem("w0_loaded")
        w_loaded = sem("w_loaded")
        const_loaded = sem("const_loaded")
        w0_hi = sem("w0_hi")
        w0_ready = sem("w0_ready")
        wq_scaled = sem("wq_scaled")
        w_hi = sem("w_hi")
        w_ready = sem("w_ready")
        x0_loaded = [sem(f"x0_loaded{i}") for i in range(2)]
        x0_hi = sem("x0_hi")
        x0_split = sem("x0_split")
        y_product = sem("y_product")
        y_hi = sem("y_hi")
        y_ready = sem("y_ready")
        a_loaded = [sem(f"a_loaded{i}") for i in range(AC)]
        a_hi = sem("a_hi")
        a_ready = sem("a_ready")
        a_used = sem("a_used")
        agg_read = sem("agg_read")
        agg_biased = sem("agg_biased")
        x_loaded = [sem(f"x_loaded{i}") for i in range(2)]
        x_added = sem("x_added")
        x1b_ready = sem("x1b_ready")
        x1_stored = [sem(f"x1_stored{i}") for i in range(2)]
        x1b_stored = [sem(f"x1b_stored{i}") for i in range(2)]
        g_loaded = [sem(f"g_loaded{i}") for i in range(2)]
        g_transposed = sem("g_transposed")
        g_hi = sem("g_hi")
        g_split = sem("g_split")
        g_used = sem("g_used")
        qkv_product = sem("qkv_product")
        q_biased = sem("q_biased")
        qkv_hi = sem("qkv_hi")
        qkv_ready = sem("qkv_ready")
        q_stored = [sem(f"q_stored{i}") for i in range(2)]
        q_loaded = [sem(f"q_loaded{i}") for i in range(2)]
        adj_loaded = [sem(f"adj_loaded{i}") for i in range(SC - 1)]
        p_dealt = [sem(f"p_dealt{i}") for i in range(QUADS)]
        x1b_loaded = [sem(f"x1b_loaded{i}") for i in range(2)]
        s_product = sem("s_product")
        s_ready = sem("s_ready")
        max_found = sem("max_found")
        max_ready = sem("max_ready")
        p_ready = sem("p_ready")
        pT_raw = sem("pT_raw")
        pT_hi = sem("pT_hi")
        pT_ready = sem("pT_ready")
        pv_done = sem("pv_done")
        sum_moved = sem("sum_moved")
        sum_found = sem("sum_found")
        sum_inverted = sem("sum_inverted")
        o_half = sem("o_half")
        o_read = sem("o_read")
        out_stored = [sem(f"out_stored{i}") for i in range(2)]
        ln_stats = sem("ln_stats")
        ln_mean = sem("ln_mean")
        ln_eps = sem("ln_eps")
        ln_shifted = sem("ln_shifted")
        ln_seed = sem("ln_seed")
        ln_newton = sem("ln_newton")
        ln_done = sem("ln_done")

        held = {name: sem(f"held_{name}") for name in ("sync", "vector", "gpsimd")}

        def hold(engine, name, semaphore, value):
            engine.wait_ge(semaphore, value)
            engine.sem_inc(held[name], 1)

        block = ctx.enter_context(nc.Block())

        def by_quadrant(bank):
            return bank.rearrange("p (a n) -> p a n", a=QUADS)

        def k_nodes(i, slot, part, half):
            return (k_split[:, part, half, :].rearrange("p (a n) -> p a n", a=QUADS)
                    [:, :, bass.ds((2 * i + slot) * P, P)])

        @block.sync
        def _(sp):
            sp.dma_start(w_raw[:, 0], w0T).then_inc(w0_loaded, 16)

            def load_x0(i, slot, again):
                if again:
                    sp.wait_ge(x0_split, 2 * i + slot - 1)
                sp.dma_start(x0_raw[:, slot], xT[2 * i + slot]).then_inc(x0_loaded[slot], 16)

            load_x0(0, 0, False)
            load_x0(0, 1, False)
            for n, w in enumerate((wqT, wkT, wvT)):
                sp.dma_start(w_raw[:, n + 1], w).then_inc(w_loaded, 16)
            sp.dma_start(b0_all[:, :], b0.partition_broadcast(P)).then_inc(const_loaded, 16)
            sp.dma_start(bv_all[:, :], bv.partition_broadcast(P)).then_inc(const_loaded, 16)
            sp.dma_start(bq_raw[:, :], bq).then_inc(const_loaded, 16)
            sp.dma_start(bk_col[:, :], bk).then_inc(const_loaded, 16)
            sp.dma_start(ident[:, :], eye).then_inc(const_loaded, 16)
            sp.dma_start(to_tile[:, :], reorder).then_inc(const_loaded, 16)
            for c in range(AC):
                sp.dma_start(a_raw[:, c], adjT[0][:, c]).then_inc(a_loaded[c], 16)
            for slot in range(2):
                sp.dma_start(resid[:, slot], x[slot]).then_inc(x_loaded[slot], 16)
            with sp.Fori(1, GROUPS // 2) as i:
                for slot in range(2):
                    load_x0(i, slot, True)

            def load_a(t):
                for c in range(AC):
                    sp.wait_ge(a_ready, AC * (t - 1) + c + 1)
                    sp.dma_start(a_raw[:, c], adjT[t][:, c]).then_inc(a_loaded[c], 16)

            load_a(1)
            with sp.Fori(1, TILES // 2) as i:
                for slot in range(2):
                    load_a(2 * i + slot)
                    sp.wait_ge(x_added, 2 * i + slot - 1)
                    sp.dma_start(resid[:, slot], x[2 * i + slot]).then_inc(x_loaded[slot], 16)

            sp.wait_ge(a_ready, AC * TILES)

            def load_group(i, slot, again):
                g = 2 * i + slot
                if again:
                    sp.wait_ge(g_transposed, HALVES * (g - 1))
                for s in range(2):
                    sp.wait_ge(x1_stored[s], 16 * GT // 2 * (g + 1))
                sp.dma_start(x1_group[:, slot], x1_dram[bass.ds(GT * g, GT)].rearrange("i p d -> p i d")
                             ).then_inc(g_loaded[slot], 16)

            load_group(0, 0, False)
            load_group(0, 1, False)
            with sp.Fori(1, GROUPS // 2) as i:
                for slot in range(2):
                    load_group(i, slot, True)

            def load_adj(t, c):
                sp.dma_start(adj_ring[:, c % (SC - 1)], adj[t][:, bass.ds(c * SCW, SCW)]
                             ).then_inc(adj_loaded[c % (SC - 1)], 16)

            load_adj(0, 0)
            load_adj(0, 1)
            sp.wait_ge(qkv_ready, 6 * (GROUPS - 1) + HALVES)
            load_adj(0, 2)
            for slot in range(2):
                sp.wait_ge(q_stored[slot], 16 * GT)
            for slot in range(2):
                sp.dma_start(q_tile[:, slot].bitcast(F32), q_dram[slot]).then_inc(q_loaded[slot], 16)
            sp.wait_ge(x_added, TILES)
            for slot in range(2):
                sp.wait_ge(x1b_stored[slot], 16 * TILES // 2)
            for slot in range(2):
                sp.dma_start(resid[:, slot], x1b_dram[slot]).then_inc(x1b_loaded[slot], 16)
                sp.wait_ge(q_stored[slot], 16 * GT * GROUPS // 2)

            def feed(i, slot, before, last):
                t = 2 * i + slot
                sp.wait_ge(s_ready, SC * t + 1)
                load_adj(t, SC - 1)
                if not last:
                    if before >= 1:
                        sp.wait_ge(s_product, SC * t)
                        sp.dma_start(q_tile[:, 1 - slot].bitcast(F32), q_dram[t + 1]
                                     ).then_inc(q_loaded[1 - slot], 16)
                    for c in (1, 2, 0):
                        hold(sp, "sync", s_ready, SC * t + (c + 1 if c else SC))
                        load_adj(t + 1, c)
                for a in range(QUADS):
                    if a == 0 and before >= 1:
                        sp.wait_ge(pT_raw, PC * t)
                    sp.wait_ge(p_ready, SC * t + a + 1)
                    sp.dma_start(dealt[a * S:(a + 1) * S], scores[:, a * QW:(a + 1) * QW]).then_inc(p_dealt[a], 16)
                if before >= 2:
                    sp.wait_ge(o_read, t - 1)
                    sp.dma_start(resid[:, slot], x1b_dram[t]).then_inc(x1b_loaded[slot], 16)

            feed(0, 0, 0, False)
            feed(0, 1, 1, False)
            with sp.Fori(1, TILES // 2 - 1) as i:
                feed(i, 0, 2, False)
                feed(i, 1, 2, False)
            feed(TILES // 2 - 1, 0, 2, False)
            feed(TILES // 2 - 1, 1, 2, True)

        @block.tensor
        def _(pe):
            def three_passes(bank, left, right, first, last):
                pe.matmul(bank, left(HI), right(HI), start=first, stop=False)
                pe.matmul(bank, left(HI), right(LO), start=False, stop=False)
                return pe.matmul(bank, left(LO), right(HI), start=False, stop=last)

            def project_rows(bank, slot, pair, w):
                for k in range(2):
                    rows = slice((2 * pair + k) * P, (2 * pair + k + 1) * P)
                    for h in range(HALVES):
                        done = three_passes(bank[:, k * D:(k + 1) * D],
                                            lambda part: xT_split[:, slot, part, h, rows],
                                            lambda part: w(part, h),
                                            h == 0, h == HALVES - 1)
                return done

            pe.wait_ge(w0_ready, 1)

            def y_group(i, slot, again):
                g = 2 * i + slot
                pe.wait_ge(x0_split, g + 1)
                for pair in range(2):
                    bank = s_bank[2 * slot + pair]
                    if again:
                        pe.wait_ge(y_ready, 2 * (g - 2) + pair + 1)
                    project_rows(bank, slot, pair, lambda part, h: w0_split[:, part, h, :]).then_inc(y_product, 1)

            y_group(0, 0, False)
            y_group(0, 1, False)
            with pe.Fori(1, GROUPS // 2) as i:
                y_group(i, 0, True)
                y_group(i, 1, True)

            pe.wait_ge(y_ready, 2 * GROUPS)

            def aggregate(t, slot, again):
                if again:
                    pe.wait_ge(agg_read, t - 1)
                for c in range(AC):
                    pe.wait_ge(a_ready, AC * t + c + 1)
                    for j in range(JA):
                        jt = c * JA + j
                        cols = slice(j * P, (j + 1) * P)
                        pe.matmul(o_bank[slot][:, :], a_split[:, slot, c, HI, cols], rhs_split[:, jt, :, :],
                                  start=(jt == 0), stop=False)
                        done = pe.matmul(o_bank[slot][:, D:2 * D], a_split[:, slot, c, LO, cols],
                                         rhs_split[:, jt, HI, :], start=False, stop=(jt == TILES - 1))
                    done.then_inc(a_used, 1)

            aggregate(0, 0, False)
            aggregate(1, 1, False)
            with pe.Fori(1, TILES // 2) as i:
                aggregate(2 * i, 0, True)
                aggregate(2 * i + 1, 1, True)

            result_bank = s_bank + [o[:, :] for o in o_bank]
            pe.wait_ge(const_loaded, 96)
            pe.wait_ge(w_ready, 3)

            def transpose_group(i, slot, again):
                g = 2 * i + slot
                pe.wait_ge(g_loaded[slot], 16 * (i + 1))
                for h in range(HALVES):
                    if again:
                        pe.wait_ge(g_split, HALVES * (g - 1) + h + 1)
                    for k in range(GT):
                        done = pe.transpose(t_bank[h][:, k * P:(k + 1) * P],
                                            x1_group[:, slot, k, h * P:(h + 1) * P], ident[:, :])
                    done.then_inc(g_transposed, 1)

            def project_columns(i, slot, which, again):
                g = 2 * i + slot
                for half in range(HALVES):
                    r = 2 * which + half
                    if again:
                        pe.wait_ge(qkv_ready, 6 * (g - 1) + r + 1)
                    feats = slice(half * P, (half + 1) * P)
                    for h in range(HALVES):
                        done = three_passes(result_bank[r],
                                            lambda part: w_split[:, which, part, h, feats],
                                            lambda part: (
                                                xT_split[:, slot, part, h, :] if which == 0 else
                                                xT_split[:, slot, part, h, :].rearrange(
                                                    "p (w a j) -> p a w j", w=GT, a=QUADS)),
                                            h == 0, h == HALVES - 1)
                    done.then_inc(qkv_product, 1)

            def project_v(i, slot, again):
                g = 2 * i + slot
                for pair in range(2):
                    r = 4 + pair
                    if again:
                        pe.wait_ge(qkv_ready, 6 * (g - 1) + r + 1)
                    elif pair == 0:
                        pe.wait_ge(agg_read, TILES)
                    project_rows(result_bank[r], slot, pair,
                                 lambda part, h: w_split[:, 2, part, h, :]).then_inc(qkv_product, 1)

            def qkv_group(i, slot, again, last):
                g = 2 * i + slot
                pe.wait_ge(g_split, HALVES * (g + 1))
                project_columns(i, slot, 0, again)
                if not last:
                    transpose_group(i + slot, 1 - slot, True)
                project_columns(i, slot, 1, again)
                project_v(i, slot, again)

            transpose_group(0, 0, False)
            qkv_group(0, 0, False, False)
            qkv_group(0, 1, True, False)
            with pe.Fori(1, GROUPS // 2 - 1) as i:
                qkv_group(i, 0, True, False)
                qkv_group(i, 1, True, False)
            qkv_group(GROUPS // 2 - 1, 0, True, False)
            qkv_group(GROUPS // 2 - 1, 1, True, True)

            def score(i, slot, again):
                t = 2 * i + slot
                pe.wait_ge(q_loaded[slot], 16 * (i + 1))
                for c in range(SC):
                    if again or c >= 2:
                        pe.wait_ge(s_ready, SC * t + c - 1)
                    for b in range(2):
                        cols = slice((2 * c + b) * BANK, (2 * c + b + 1) * BANK)
                        for h in range(HALVES):
                            done = three_passes(s_bank[2 * (c % 2) + b],
                                                lambda part: q_tile[:, slot, part, h, :],
                                                lambda part: k_split[:, part, h, cols],
                                                h == 0, h == HALVES - 1)
                    done.then_inc(s_product, 1)

            def move_sums(t, slot, again):
                pe.wait_ge(p_ready, SC * (t + 1))
                if again:
                    pe.wait_ge(sum_found, t - 1)
                pe.matmul(t_bank[slot][:, 0:SC], to_tile[:, :], row_sum_of[:, slot, :],
                          start=True, stop=True).then_inc(sum_moved, 1)

            def attend(t, slot, again):
                if again:
                    pe.wait_ge(o_read, t - 1)
                for c in range(HC):
                    pe.wait_ge(pT_ready, HC * t + c + 1)
                    for k in range(GT):
                        jt = c * GT + k
                        pe.matmul(o_bank[slot][:, :], pT_split[:, c % 4, HI, k, :], rhs_split[:, jt, :, :],
                                  start=(jt == 0), stop=False)
                        done = pe.matmul(o_bank[slot][:, D:2 * D], pT_split[:, c % 4, LO, k, :],
                                         rhs_split[:, jt, HI, :], start=False, stop=(jt == TILES - 1))
                    done.then_inc(pv_done, 1)

            pe.wait_ge(qkv_ready, 6 * (GROUPS - 1) + 4)
            score(0, 0, False)
            score(0, 1, True)
            move_sums(0, 0, False)
            pe.wait_ge(qkv_ready, 6 * GROUPS)
            attend(0, 0, False)
            score(1, 0, True)
            move_sums(1, 1, False)
            attend(1, 1, False)

            def step(i, slot):
                t = 2 * i + slot
                move_sums(t, slot, True)
                score(i + slot, 1 - slot, True)
                attend(t, slot, True)

            with pe.Fori(1, TILES // 2 - 1) as i:
                step(i, 0)
                step(i, 1)
            step(TILES // 2 - 1, 0)
            move_sums(TILES - 1, 1, True)
            attend(TILES - 1, 1, True)

        @block.scalar
        def _(act):
            act.wait_ge(w0_loaded, 16)
            act.activation(w0_split[:, HI], w_raw[:, 0], ACT.Copy).then_inc(w0_hi, 1)

            def y_group(i, slot, again):
                g = 2 * i + slot
                act.wait_ge(x0_loaded[slot], 16 * (i + 1))
                if again:
                    act.wait_ge(y_product, 2 * (g - 1))
                act.activation(xT_split[:, slot, HI], x0_raw[:, slot], ACT.Copy).then_inc(x0_hi, 1)

            def y_rows(i, slot):
                for pair in range(2):
                    act.wait_ge(y_product, 2 * (2 * i + slot) + pair + 1)
                    act.activation(rhs_split[:, bass.ds(GT * (2 * i + slot) + 2 * pair, 2), HI, :],
                                   s_bank[2 * slot + pair].rearrange("p (k d) -> p k d", k=2),
                                   ACT.Copy).then_inc(y_hi, 1)

            y_group(0, 0, False)
            y_group(0, 1, False)
            with act.Fori(1, GROUPS // 2) as i:
                y_rows(i - 1, 0)
                y_group(i, 0, True)
                y_rows(i - 1, 1)
                y_group(i, 1, True)
            y_rows(GROUPS // 2 - 1, 0)
            y_rows(GROUPS // 2 - 1, 1)

            def a_tile(i, slot, again):
                t = 2 * i + slot
                for c in range(AC):
                    act.wait_ge(a_loaded[c], 16 * (t + 1))
                    if again:
                        act.wait_ge(a_used, AC * (t - 2) + c + 1)
                    act.activation(a_split[:, slot, c, HI], a_raw[:, c], ACT.Copy).then_inc(a_hi, 1)

            a_tile(0, 0, False)
            a_tile(0, 1, False)
            act.wait_ge(wq_scaled, 1)
            for n in range(3):
                act.activation(w_split[:, n, HI], w_raw[:, n + 1], ACT.Copy).then_inc(w_hi, 1)
            with act.Fori(1, TILES // 2) as i:
                a_tile(i, 0, True)
                a_tile(i, 1, True)

            result_bank = s_bank + [o[:, :] for o in o_bank]

            def group_hi(i, slot, again):
                g = 2 * i + slot
                for h in range(HALVES):
                    act.wait_ge(g_transposed, HALVES * g + h + 1)
                    if again:
                        act.wait_ge(qkv_product, 6 * (g - 1))
                    act.activation(xT_split[:, slot, HI, h], t_bank[h][:, :], ACT.Copy).then_inc(g_hi, 1)

            def result_hi(i, slot, r, again):
                g = 2 * i + slot
                act.wait_ge(qkv_product, 6 * g + r + 1)
                if r < 2:
                    if again:
                        act.wait_ge(q_stored[slot], 16 * GT * i)
                    act.activation(q_raw[:, r, :].rearrange("p (w i s) -> p w s i", w=GT, s=QUADS),
                                   result_bank[r].rearrange("p (w s i) -> p w s i", w=GT, s=QUADS),
                                   ACT.Identity, bias=bq_col[:, r:r + 1]).then_inc(q_biased, 1)
                    act.wait_ge(q_biased, HALVES * g + r + 1)
                    act.activation(q_stage[:, slot, HI, r], q_raw[:, r, :], ACT.Copy).then_inc(qkv_hi, 1)
                elif r < 4:
                    act.activation(k_nodes(i, slot, HI, r - 2), by_quadrant(result_bank[r]), ACT.Identity,
                                   bias=bk_col[:, r - 2:r - 1]).then_inc(qkv_hi, 1)
                else:
                    act.activation(rhs_split[:, bass.ds(GT * g + 2 * (r - 4), 2), HI, :],
                                   result_bank[r].rearrange("p (k d) -> p k d", k=2),
                                   ACT.Copy).then_inc(qkv_hi, 1)

            def qkv_group(i, slot, again, last):
                for r in range(2):
                    result_hi(i, slot, r, again)
                if not last:
                    group_hi(i + slot, 1 - slot, again or slot == 1)
                for r in range(2, 6):
                    result_hi(i, slot, r, again)

            group_hi(0, 0, False)
            qkv_group(0, 0, False, False)
            qkv_group(0, 1, False, False)
            with act.Fori(1, GROUPS // 2 - 1) as i:
                qkv_group(i, 0, True, False)
                qkv_group(i, 1, True, False)
            qkv_group(GROUPS // 2 - 1, 0, True, False)
            qkv_group(GROUPS // 2 - 1, 1, True, True)

            def exp(t, slot, c):
                if c == 0:
                    act.wait_ge(max_ready, t + 1)
                s = scores[:, c * SCW:(c + 1) * SCW]
                act.activation(s, s, ACT.Exp, bias=neg_max[:, slot, :], scale=2.0,
                               accum_out=row_sum_of[:, slot, c:c + 1]).then_inc(p_ready, 1)

            def pT_hi_part(t, c, again):
                act.wait_ge(pT_raw, PC * t + c // 2 + 1)
                if again or c >= 4:
                    act.wait_ge(pv_done, HC * t + c - 3)
                act.activation(pT_split[:, c % 4, HI], pT[:, c // 2 % 2, c % 2 * GT:(c % 2 + 1) * GT],
                               ACT.Copy).then_inc(pT_hi, 1)

            def step(t, slot, before, last):
                for c in range(4):
                    pT_hi_part(t, c, before >= 1)
                pT_hi_part(t, 4, True)
                for c in range(SC):
                    if not last:
                        exp(t + 1, 1 - slot, c)
                    if c >= 1:
                        pT_hi_part(t, 4 + c, True)

            for c in range(SC):
                exp(0, 0, c)
            step(0, 0, 0, False)
            step(1, 1, 1, False)
            with act.Fori(1, TILES // 2 - 1) as i:
                step(2 * i, 0, 2, False)
                step(2 * i + 1, 1, 2, False)
            step(TILES - 2, 0, 2, False)
            step(TILES - 1, 1, 2, True)

        @block.vector
        def _(dve):
            def norm_stats(n, slot, again):
                dve.bn_stats(stats[:, :], acc[:, slot, :]).then_inc(ln_stats, 1)
                if again:
                    dve.wait_ge(ln_done, n - 1)
                hold(dve, "vector", ln_stats, n + 1)
                dve.bn_aggr(mean_var[:, slot, :], stats[:, :]).then_inc(ln_mean, 1)
                dve.wait_ge(ln_mean, n + 1)
                dve.tensor_scalar(var_eps[:, slot, :], mean_var[:, slot, 1:2], EPS, None, ALU.add).then_inc(ln_eps, 1)
                dve.wait_ge(ln_eps, n + 1)
                dve.tensor_scalar(half_bits[:, :].bitcast(I32), var_eps[:, slot, :].bitcast(I32), 1, None,
                                  ALU.logical_shift_right).then_inc(ln_shifted, 1)
                dve.wait_ge(ln_shifted, n + 1)
                dve.tensor_scalar(guess[:, slot, :].bitcast(I32), half_bits[:, :].bitcast(I32), -1.0,
                                  float(RSQRT_MAGIC), ALU.mult, ALU.add).then_inc(ln_seed, 1)

            def lo_part(out, whole, hi):
                return dve.tensor_tensor(out, whole, hi.bitcast(F32), ALU.subtract)

            dve.wait_ge(w0_hi, 1)
            lo_part(w0_split[:, LO], w_raw[:, 0], w0_split[:, HI]).then_inc(w0_ready, 1)

            def y_group(i, slot):
                dve.wait_ge(x0_hi, 2 * i + slot + 1)
                lo_part(xT_split[:, slot, LO], x0_raw[:, slot], xT_split[:, slot, HI]).then_inc(x0_split, 1)

            def y_rows(i, slot):
                for pair in range(2):
                    dve.wait_ge(y_hi, 2 * (2 * i + slot) + pair + 1)
                    rows = bass.ds(GT * (2 * i + slot) + 2 * pair, 2)
                    lo_part(rhs_split[:, rows, LO, :],
                            s_bank[2 * slot + pair].rearrange("p (k d) -> p k d", k=2),
                            rhs_split[:, rows, HI, :]).then_inc(y_ready, 1)

            y_group(0, 0)
            y_group(0, 1)
            with dve.Fori(1, GROUPS // 2) as i:
                y_rows(i - 1, 0)
                y_group(i, 0)
                y_rows(i - 1, 1)
                y_group(i, 1)
            y_rows(GROUPS // 2 - 1, 0)
            y_rows(GROUPS // 2 - 1, 1)

            scale = 0.5 * D ** -0.5
            dve.wait_ge(const_loaded, 96)
            dve.tensor_scalar(bq_col[:, :], bq_raw[:, :], scale, None, ALU.mult)
            dve.tensor_scalar(w_raw[:, 1], w_raw[:, 1], scale, None, ALU.mult).then_inc(wq_scaled, 1)

            def a_tile(t, slot):
                for c in range(AC):
                    dve.wait_ge(a_hi, AC * t + c + 1)
                    lo_part(a_split[:, slot, c, LO], a_raw[:, c], a_split[:, slot, c, HI]).then_inc(a_ready, 1)

            def first_layer(i, slot, again):
                t = 2 * i + slot
                if again:
                    dve.wait_ge(ln_done, t - 1)
                dve.wait_ge(a_used, AC * (t + 1))
                dve.tensor_tensor(acc[:, slot, :], o_bank[slot][:, D:2 * D], b0_all[:, :], ALU.add
                                  ).then_inc(agg_biased, 1)
                dve.wait_ge(agg_biased, t + 1)
                dve.tensor_tensor(acc[:, slot, :], o_bank[slot][:, 0:D], acc[:, slot, :], ALU.add
                                  ).then_inc(agg_read, 1)
                dve.wait_ge(agg_read, t + 1)
                dve.wait_ge(x_loaded[slot], 16 * (i + 1))
                dve.scalar_tensor_tensor(out=acc[:, slot, :], in0=acc[:, slot, :], scalar=0.0,
                                         in1=resid[:, slot, :], op0=ALU.max, op1=ALU.add).then_inc(x_added, 1)
                dve.wait_ge(x_added, t + 1)
                norm_stats(t, slot, again)

            a_tile(0, 0)
            a_tile(1, 1)
            for n in range(3):
                dve.wait_ge(w_hi, n + 1)
                lo_part(w_split[:, n, LO], w_raw[:, n + 1], w_split[:, n, HI]).then_inc(w_ready, 1)
            first_layer(0, 0, False)
            a_tile(2, 0)
            first_layer(0, 1, False)
            a_tile(3, 1)
            with dve.Fori(1, TILES // 2 - 1) as i:
                first_layer(i, 0, True)
                a_tile(2 * i + 2, 0)
                first_layer(i, 1, True)
                a_tile(2 * i + 3, 1)
            first_layer(TILES // 2 - 1, 0, True)

            result_bank = s_bank + [o[:, :] for o in o_bank]

            def group_lo(i, slot):
                g = 2 * i + slot
                for h in range(HALVES):
                    dve.wait_ge(g_hi, HALVES * g + h + 1)
                    lo_part(xT_split[:, slot, LO, h], t_bank[h][:, :], xT_split[:, slot, HI, h]).then_inc(g_split, 1)

            def result_lo(i, slot, r):
                g = 2 * i + slot
                dve.wait_ge(qkv_hi, 6 * g + r + 1)
                if r < 2:
                    lo_part(q_stage[:, slot, LO, r], q_raw[:, r, :], q_stage[:, slot, HI, r]).then_inc(qkv_ready, 1)
                elif r < 4:
                    dve.scalar_tensor_tensor(out=k_nodes(i, slot, LO, r - 2), in0=by_quadrant(result_bank[r]),
                                             scalar=bk_col[:, r - 2:r - 1],
                                             in1=k_nodes(i, slot, HI, r - 2).bitcast(F32),
                                             op0=ALU.add, op1=ALU.subtract).then_inc(qkv_ready, 1)
                else:
                    rows = bass.ds(GT * g + 2 * (r - 4), 2)
                    lo_part(rhs_split[:, rows, LO, :], result_bank[r].rearrange("p (k d) -> p k d", k=2),
                            rhs_split[:, rows, HI, :]).then_inc(qkv_ready, 1)

            def qkv_group(i, slot, last):
                for r in range(2):
                    result_lo(i, slot, r)
                if not last:
                    group_lo(i + slot, 1 - slot)
                for r in range(2, 6):
                    result_lo(i, slot, r)

            group_lo(0, 0)
            first_layer(TILES // 2 - 1, 1, True)
            with dve.Fori(0, GROUPS // 2 - 1) as i:
                qkv_group(i, 0, False)
                qkv_group(i, 1, False)
            qkv_group(GROUPS // 2 - 1, 0, False)
            qkv_group(GROUPS // 2 - 1, 1, True)

            def add_adj(i, slot, c, again):
                t = 2 * i + slot
                if c % (SC - 1) == 0:
                    dve.wait_ge(adj_loaded[0], 32 * t + (16 if c == 0 else 32))
                else:
                    dve.wait_ge(adj_loaded[c], 16 * (t + 1))
                if again:
                    dve.wait_ge(p_dealt[c], 16 * t)
                hold(dve, "vector", s_product, SC * t + c + 1)
                dve.tensor_tensor_reduce(out=scores[:, c * SCW:(c + 1) * SCW],
                                         in0=s_pair[c % 2].rearrange("p b n -> p (b n)"),
                                         in1=adj_ring[:, c % (SC - 1), :],
                                         scale=1.0, scalar=-3.0e38, op0=ALU.add, op1=ALU.max,
                                         accum_out=row_max_of[:, c:c + 1]).then_inc(s_ready, 1)

            def whole_max(t, slot):
                dve.wait_ge(s_ready, SC * (t + 1))
                dve.tensor_reduce(row_max[:, :], row_max_of[:, :], AX_X, ALU.max).then_inc(max_found, 1)
                dve.wait_ge(max_found, t + 1)
                dve.tensor_scalar(neg_max[:, slot, :], row_max[:, :], -2.0, None, ALU.mult).then_inc(max_ready, 1)

            def transpose_p(t, c, again):
                if again or c >= 2:
                    dve.wait_ge(pT_ready, HC * t + 2 * c - 2)
                if c == 0:
                    for a in range(QUADS):
                        dve.wait_ge(p_dealt[a], 16 * (t + 1))
                dve.transpose(pT[:, c % 2].rearrange("p w (q i) -> p q w i", q=QUADS),
                              dealt[:, :, c * CT * S:(c + 1) * CT * S].rearrange("p q (w i) -> p q w i", i=S)
                              ).then_inc(pT_raw, 1)

            def pT_lo(t, c):
                dve.wait_ge(pT_hi, HC * t + c + 1)
                lo_part(pT_split[:, c % 4, LO], pT[:, c // 2 % 2, c % 2 * GT:(c % 2 + 1) * GT],
                        pT_split[:, c % 4, HI]).then_inc(pT_ready, 1)

            def invert_sum(t, slot):
                dve.wait_ge(sum_moved, t + 1)
                dve.tensor_reduce(row_sum[:, :], t_bank[slot][:, 0:SC], AX_X, ALU.add).then_inc(sum_found, 1)
                dve.wait_ge(sum_found, t + 1)
                dve.reciprocal(inv_sum[:, slot, :], row_sum[:, :]).then_inc(sum_inverted, 1)

            def residual(i, slot):
                t = 2 * i + slot
                dve.wait_ge(sum_inverted, t + 1)
                dve.wait_ge(ln_done, TILES + t - 1)
                dve.wait_ge(pv_done, HC * (t + 1))
                dve.wait_ge(x1b_loaded[slot], 16 * (i + 1))
                dve.scalar_tensor_tensor(out=acc[:, slot, :], in0=o_bank[slot][:, D:2 * D],
                                         scalar=inv_sum[:, slot, :], in1=resid[:, slot, :],
                                         op0=ALU.mult, op1=ALU.add).then_inc(o_half, 1)
                dve.wait_ge(o_half, t + 1)
                dve.scalar_tensor_tensor(out=acc[:, slot, :], in0=o_bank[slot][:, 0:D],
                                         scalar=inv_sum[:, slot, :], in1=acc[:, slot, :],
                                         op0=ALU.mult, op1=ALU.add).then_inc(o_read, 1)

            def residual_stats(i, slot):
                t = 2 * i + slot
                dve.wait_ge(o_read, t + 1)
                norm_stats(TILES + t, slot, True)

            def step(i, slot, before, last):
                t = 2 * i + slot
                behind, ahead = (i - 1 + slot, 1 - slot), (i + slot, 1 - slot)
                transpose_p(t, 0, before >= 1)
                transpose_p(t, 1, before >= 1)
                if not last:
                    add_adj(*ahead, 0, True)
                pT_lo(t, 0)
                pT_lo(t, 1)
                if not last:
                    add_adj(*ahead, 1, True)
                transpose_p(t, 2, True)
                if not last:
                    add_adj(*ahead, 2, True)
                pT_lo(t, 2)
                pT_lo(t, 3)
                if not last:
                    add_adj(*ahead, 3, True)
                    whole_max(t + 1, 1 - slot)
                transpose_p(t, 3, True)
                pT_lo(t, 4)
                invert_sum(t, slot)
                pT_lo(t, 5)
                if before >= 1:
                    residual(*behind)
                pT_lo(t, 6)
                pT_lo(t, 7)
                if before >= 1:
                    residual_stats(*behind)

            for slot in range(2):
                dve.wait_ge(q_stored[slot], 16 * GT * GROUPS // 2)
            for slot in range(2):
                dve.wait_ge(x1b_stored[slot], 16 * TILES // 2)
            for c in range(SC):
                add_adj(0, 0, c, False)
            whole_max(0, 0)
            step(0, 0, 0, False)
            step(0, 1, 1, False)
            with dve.Fori(1, TILES // 2 - 1) as i:
                step(i, 0, 2, False)
                step(i, 1, 2, False)
            step(TILES // 2 - 1, 0, 2, False)
            step(TILES // 2 - 1, 1, 2, True)
            residual(TILES // 2 - 1, 1)
            residual_stats(TILES // 2 - 1, 1)

        @block.gpsimd
        def _(pool):
            pool.wait_ge(const_loaded, 96)

            def normalise(n, slot):
                hold(pool, "gpsimd", ln_seed, n + 1)
                r = guess[:, slot, :]
                for k in range(NEWTON_STEPS):
                    before = 4 * NEWTON_STEPS * n + 4 * k
                    pool.tensor_tensor(newton_a[:, :], r, r, ALU.mult).then_inc(ln_newton, 1)
                    pool.wait_ge(ln_newton, before + 1)
                    pool.tensor_tensor(newton_a[:, :], newton_a[:, :], var_eps[:, slot, :], ALU.mult
                                       ).then_inc(ln_newton, 1)
                    hold(pool, "gpsimd", ln_newton, before + 2)
                    pool.tensor_scalar(newton_a[:, :], newton_a[:, :], -0.5, 1.5, ALU.mult, ALU.add
                                       ).then_inc(ln_newton, 1)
                    pool.wait_ge(ln_newton, before + 3)
                    pool.tensor_tensor(rstd[:, :], r, newton_a[:, :], ALU.mult).then_inc(ln_newton, 1)
                    r = rstd[:, :]
                    if k < NEWTON_STEPS - 1:
                        pool.wait_ge(ln_newton, before + 4)
                hold(pool, "gpsimd", ln_newton, 4 * NEWTON_STEPS * (n + 1))
                pool.tensor_scalar(normed[:, slot, :], acc[:, slot, :], mean_var[:, slot, 0:1], rstd[:, :],
                                   ALU.subtract, ALU.mult).then_inc(ln_done, 1)

            def keep_x1(i, slot, again):
                t = 2 * i + slot
                if again:
                    pool.wait_ge(x1_stored[slot], 16 * i)
                    pool.wait_ge(x1b_stored[slot], 16 * i)
                normalise(t, slot)
                pool.wait_ge(ln_done, t + 1)
                pool.tensor_tensor(x1b[:, slot, :], normed[:, slot, :], bv_all[:, :], ALU.add).then_inc(x1b_ready, 1)
                pool.dma_start(x1_dram[t], normed[:, slot, :]).then_inc(x1_stored[slot], 16)
                hold(pool, "gpsimd", x1b_ready, t + 1)
                pool.dma_start(x1b_dram[t], x1b[:, slot, :]).then_inc(x1b_stored[slot], 16)

            keep_x1(0, 0, False)
            keep_x1(0, 1, False)
            with pool.Fori(1, TILES // 2) as i:
                keep_x1(i, 0, True)
                keep_x1(i, 1, True)

            with pool.Fori(0, GROUPS // 2) as i:
                for slot in range(2):
                    g = 2 * i + slot
                    hold(pool, "gpsimd", qkv_ready, 6 * g + HALVES)
                    for k in range(GT):
                        pool.dma_start(q_dram[GT * g + k].rearrange("p s h n -> p (s h) n"),
                                       q_stage[:, slot].bitcast(F32).rearrange("p s h n -> p (s h) n")[:, :, k * P:(k + 1) * P]
                                       ).then_inc(q_stored[slot], 16)

            for slot in range(2):
                pool.wait_ge(x1_stored[slot], 16 * TILES // 2)

            def finish(i, slot, again):
                t = 2 * i + slot
                if again:
                    pool.wait_ge(out_stored[slot], 16 * i)
                normalise(TILES + t, slot)
                hold(pool, "gpsimd", ln_done, TILES + t + 1)
                pool.dma_start(out[t], normed[:, slot, :]).then_inc(out_stored[slot], 16)

            finish(0, 0, False)
            finish(0, 1, False)
            with pool.Fori(1, TILES // 2) as i:
                finish(i, 0, True)
                finish(i, 1, True)
            for slot in range(2):
                pool.wait_ge(out_stored[slot], 16 * TILES // 2)


def kernel(x, adj, L0_gnn_W, L0_gnn_b, L1_gnn_Wq, L1_gnn_bq, L1_gnn_Wk, L1_gnn_bk, L1_gnn_Wv, L1_gnn_bv):
    import numpy as np
    import concourse.bacc as bacc
    from concourse.bass_utils import run_bass_kernel_spmd

    def tile_order(a):
        a = np.asarray(a)
        return a.reshape(QUADS, TILES, S, -1).transpose(1, 0, 2, 3).reshape(a.shape)

    def score_order(a):
        return a.reshape(TILES, QUADS, S, -1).transpose(0, 2, 1, 3).reshape(a.shape)

    x, adj = tile_order(x), tile_order(adj)
    adj_tiled = tile_order(adj.T).T

    def features_first(w):
        return np.ascontiguousarray(np.asarray(w).T.reshape(HALVES, P, D).transpose(1, 0, 2))

    def column(b):
        return np.ascontiguousarray(np.asarray(b).reshape(HALVES, P).T)

    arrays = {
        "xT": np.ascontiguousarray(x.reshape(GROUPS, BANK, HALVES, P).transpose(0, 3, 2, 1)),
        "x": np.ascontiguousarray(x.reshape(TILES, P, D)),
        "adjT": np.ascontiguousarray(
            adj_tiled.reshape(TILES, P, AC, JA, P).transpose(0, 4, 2, 3, 1)).reshape(TILES, P, AC, ACW),
        "adj": np.ascontiguousarray(score_order(adj)).reshape(TILES, P, N),
        "w0T": features_first(L0_gnn_W),
        "wqT": features_first(L1_gnn_Wq),
        "wkT": features_first(L1_gnn_Wk),
        "wvT": features_first(L1_gnn_Wv),
        "b0": np.ascontiguousarray(L0_gnn_b),
        "bq": column(L1_gnn_bq),
        "bk": column(L1_gnn_bk),
        "bv": np.ascontiguousarray(L1_gnn_bv),
        "eye": np.eye(P, dtype=np.float32),
        "reorder": score_order(np.tile(np.eye(P, dtype=np.float32), (TILES, 1)))[:P].copy(),
    }
    nc = bacc.Bacc("TRN2", target_bir_lowering=False, num_devices=1)
    args = [nc.dram_tensor(f"in_{name}", a.shape, mybir.dt.from_np(a.dtype), kind="ExternalInput").ap()
            for name, a in arrays.items()]
    out = nc.dram_tensor("out", (TILES, P, D), F32, kind="ExternalOutput").ap()
    two_layers(nc, *args, out)
    r = run_bass_kernel_spmd(nc, [{f"in_{name}": a for name, a in arrays.items()}], core_ids=[0])
    return np.ascontiguousarray(r.results[0]["out"].reshape(TILES, QUADS, S, D).transpose(1, 0, 2, 3)).reshape(N, D)
```

```python
import concourse.bass as bass
from concourse import mybir
from contextlib import ExitStack

N, D, P = 4096, 256, 128
TILES = N // P
HALVES = D // P
BANK = 512
GROUPS = N // BANK
GT = BANK // P
AC = 4
ACW = N // AC
JA = ACW // P
SC = 4
SCW = N // SC
HC = N // BANK
POOL_PIECES = 2
S = 32
QUADS = P // S
QW = N // QUADS
PC = 4
CT = TILES // PC
EPS = 1e-5
SCALE = D ** -0.5
HALF_SCALE = SCALE / 2
HI, LO = 0, 1
RSQRT_MAGIC = 0x5F3759DF
NEWTON_STEPS = 3

F32 = mybir.dt.float32
F32R = mybir.dt.float32r
I32 = mybir.dt.int32
ALU = mybir.AluOpType
ACT = mybir.ActivationFunctionType
AX_X = mybir.AxisListType.X


def two_layers(nc, xT, x, adjT, adj, w0T, wq, wk, wvT, b0, bq, bk, bv, eye, to_tile_in,
               to_score_in, out):
    z_dram = nc.dram_tensor("z_scratch", (TILES, P, 2, HALVES, P), F32, kind="Internal").ap()
    x1_dram = nc.dram_tensor("x1_scratch", (TILES, P, D), F32, kind="Internal").ap()
    x1b_dram = nc.dram_tensor("x1_bv_scratch", (TILES, P, D), F32, kind="Internal").ap()

    base = (nc.sbuf_base + 63) // 64 * 64
    KB = 1024
    R_RHS, R_X1T, R_SPLIT, R_Z, R_WORK, R_SMALL = (base + k * KB for k in (0, 64, 128, 144, 148, 200))

    def at(name, shape, dt, offset):
        return nc.alloc_sbuf_tensor_at(name, shape, dt, offset=offset)

    rhs_split = at("rhs_split", [P, TILES, 2, D], F32R, R_RHS)
    a_split = at("a_split", [P, 2, AC, 2, ACW], F32R, R_X1T)
    x1T_split = at("x1T_split", [P, HALVES, 2, N], F32R, R_X1T)
    xT_split = at("xT_split", [P, 2, 2, HALVES, BANK], F32R, R_SPLIT)
    pT_split = at("pT_split", [P, 4, 2, GT, P], F32R, R_SPLIT)
    w0_split = at("w0_split", [P, 2, HALVES, D], F32R, R_Z)
    z_tile = at("z_tile", [P, 2, 2, HALVES, P], F32R, R_Z)
    ident = at("ident", [P, P], F32, R_SPLIT)
    to_score = at("to_score", [P, P], F32, R_SPLIT + KB // 2)
    u_all = at("u_all", [P, D], F32, R_SPLIT + KB)
    c_product = at("c_product", [P, GT, D], F32, R_SPLIT + 4 * KB)
    w_split = at("w_split", [P, 2, 2, HALVES, D], F32R, R_SPLIT + 8 * KB)
    a_raw = at("a_raw", [P, AC, ACW], F32, R_WORK)
    w_raw = at("w_raw", [P, 4, HALVES, D], F32, R_WORK + 16 * KB)
    x0_raw = at("x0_raw", [P, GROUPS, HALVES, BANK], F32, R_X1T + 32 * KB)
    x1_group = at("x1_group", [P, 2, GT, D], F32, R_WORK)
    z_stage = at("z_stage", [P, 2, 2, HALVES, BANK], F32R, R_WORK + 8 * KB)
    z_raw = at("z_raw", [P, HALVES, BANK], F32, R_WORK + 48 * KB)
    b0_all = at("b0_all", [P, D], F32, R_WORK + 36 * KB)
    bv_all = at("bv_all", [P, D], F32, R_WORK + 37 * KB)
    x1b = at("x1b", [P, 2, D], F32, R_WORK + 38 * KB)
    scores = at("scores", [P, N], F32, R_WORK)
    dealt = at("dealt", [P, QUADS, QW], F32, R_WORK + 16 * KB)
    pT = at("pT", [P, 2, CT, P], F32, R_WORK + 32 * KB)
    adj_ring = at("adj_ring", [P, SC - 1, SCW], F32, R_WORK + 40 * KB)

    small = [R_SMALL]

    def little(name, shape, dt=F32):
        words = 1
        for n in shape[1:]:
            words *= n
        t = at(name, shape, dt, small[0])
        small[0] += (4 * words + 31) // 32 * 32
        return t

    to_tile = little("to_tile", [P, P])
    resid = little("resid", [P, 2, D])
    acc = little("acc", [P, 2, D])
    normed = little("normed", [P, 2, D])
    bq_col = little("bq_col", [P, HALVES])
    bk_col = little("bk_col", [P, HALVES])
    bz_col = little("bz_col", [P, HALVES])
    c_const = little("c_const", [P, 1])
    c_raw = little("c_raw", [P, TILES])
    c_all = little("c_all", [P, TILES])
    stats = little("stats", [P, 6])
    mean_var = little("mean_var", [P, 2, 2])
    var_eps = little("var_eps", [P, 2, 1])
    half_bits = little("half_bits", [P, 1])
    guess = little("guess", [P, 2, 1])
    newton_a = little("newton_a", [P, 1])
    half_var = little("half_var", [P, 1])
    rstd = little("rstd", [P, 1])
    row_max_of = little("row_max_of", [P, SC])
    chunk_max = little("chunk_max", [P, 1])
    row_max = little("row_max", [P, 1])
    exp_bias = little("exp_bias", [P, 2, 1])
    row_sum_of = little("row_sum_of", [P, 2, SC])
    row_sum = little("row_sum", [P, 1])
    inv_sum = little("inv_sum", [P, 2, 1])

    with ExitStack() as ctx:
        def psum(name):
            return ctx.enter_context(nc.psum_tensor(name, [P, BANK], F32))

        def sem(name):
            return ctx.enter_context(nc.semaphore(name))

        s_pair = [ctx.enter_context(nc.psum_tensor(f"s_pair{i}", [P, 2, BANK], F32)) for i in range(2)]
        s_bank = [s_pair[i // 2][:, i % 2, :] for i in range(4)]
        t_bank = [psum(f"t_bank{i}") for i in range(2)]
        o_bank = [psum(f"o_bank{i}")[:, :] for i in range(2)]

        w0_loaded = sem("w0_loaded")
        w_loaded = sem("w_loaded")
        const_loaded = sem("const_loaded")
        w0_hi = sem("w0_hi")
        w0_ready = sem("w0_ready")
        order_loaded = sem("order_loaded")
        m_product = sem("m_product")
        m_terms = sem("m_terms")
        w_hi = sem("w_hi")
        w_ready = sem("w_ready")
        x0_loaded = [sem(f"x0_loaded{i}") for i in range(2)]
        x0_hi = sem("x0_hi")
        x0_split = sem("x0_split")
        y_product = sem("y_product")
        y_hi = sem("y_hi")
        y_ready = sem("y_ready")
        a_loaded = [sem(f"a_loaded{i}") for i in range(AC)]
        a_hi = sem("a_hi")
        a_ready = sem("a_ready")
        a_used = sem("a_used")
        agg_read = sem("agg_read")
        agg_biased = sem("agg_biased")
        x_loaded = [sem(f"x_loaded{i}") for i in range(2)]
        x_added = sem("x_added")
        x1b_ready = sem("x1b_ready")
        x1_stored = [sem(f"x1_stored{i}") for i in range(2)]
        x1b_stored = [sem(f"x1b_stored{i}") for i in range(2)]
        g_loaded = [sem(f"g_loaded{i}") for i in range(2)]
        g_transposed = sem("g_transposed")
        g_hi = sem("g_hi")
        g_split = sem("g_split")
        c_multiplied = sem("c_multiplied")
        c_summed = sem("c_summed")
        c_moved = sem("c_moved")
        c_ready = sem("c_ready")
        zv_product = sem("zv_product")
        z_biased = sem("z_biased")
        zv_hi = sem("zv_hi")
        zv_ready = sem("zv_ready")
        z_stored = [sem(f"z_stored{i}") for i in range(2)]
        z_loaded = [sem(f"z_loaded{i}") for i in range(2)]
        adj_loaded = [sem(f"adj_loaded{i}") for i in range(SC - 1)]
        p_dealt = [sem(f"p_dealt{i}") for i in range(QUADS)]
        x1b_loaded = [sem(f"x1b_loaded{i}") for i in range(2)]
        s_product = sem("s_product")
        s_ready = sem("s_ready")
        max_found = sem("max_found")
        max_shifted = sem("max_shifted")
        max_ready = sem("max_ready")
        p_ready = sem("p_ready")
        pT_raw = sem("pT_raw")
        pT_hi = sem("pT_hi")
        pT_ready = sem("pT_ready")
        pv_done = sem("pv_done")
        sum_moved = sem("sum_moved")
        sum_found = sem("sum_found")
        sum_inverted = sem("sum_inverted")
        o_half = sem("o_half")
        o_read = sem("o_read")
        out_stored = [sem(f"out_stored{i}") for i in range(2)]
        last_stored = sem("last_stored")
        ln_stats = sem("ln_stats")
        ln_mean = sem("ln_mean")
        ln_eps = sem("ln_eps")
        ln_shifted = sem("ln_shifted")
        ln_seed = sem("ln_seed")
        ln_newton = sem("ln_newton")
        ln_done = sem("ln_done")
        last_newton = sem("last_newton")

        held = {name: sem(f"held_{name}") for name in ("sync", "vector", "gpsimd")}

        def hold(engine, name, semaphore, value):
            engine.wait_ge(semaphore, value)
            engine.sem_inc(held[name], 1)

        block = ctx.enter_context(nc.Block())

        @block.sync
        def _(sp):
            sp.dma_start(w_raw[:, 0], w0T).then_inc(w0_loaded, 16)

            def load_x0(i, slot, again):
                if again:
                    hold(sp, "sync", x0_loaded[slot], 16 * i)
                sp.dma_start(x0_raw[:, 2 * i + slot], xT[2 * i + slot]).then_inc(x0_loaded[slot], 16)

            load_x0(0, 0, False)
            load_x0(0, 1, False)
            with sp.Fori(1, GROUPS // 2) as i:
                for slot in range(2):
                    load_x0(i, slot, True)
            for c in range(AC):
                sp.dma_start(a_raw[:, c], adjT[0][:, c]).then_inc(a_loaded[c], 16)
            for n, w in enumerate((wq, wk, wvT)):
                sp.dma_start(w_raw[:, n + 1], w).then_inc(w_loaded, 16)
            sp.dma_start(b0_all[:, :], b0.partition_broadcast(P)).then_inc(const_loaded, 16)
            sp.dma_start(bv_all[:, :], bv.partition_broadcast(P)).then_inc(const_loaded, 16)
            sp.dma_start(bq_col[:, :], bq).then_inc(const_loaded, 16)
            sp.dma_start(bk_col[:, :], bk).then_inc(const_loaded, 16)
            sp.dma_start(to_tile[:, :], to_tile_in).then_inc(const_loaded, 16)
            for slot in range(2):
                sp.dma_start(resid[:, slot], x[slot]).then_inc(x_loaded[slot], 16)

            def load_a(t):
                for c in range(AC):
                    sp.wait_ge(a_ready, AC * (t - 1) + c + 1)
                    sp.dma_start(a_raw[:, c], adjT[t][:, c]).then_inc(a_loaded[c], 16)

            load_a(1)
            sp.wait_ge(y_product, 2 * GROUPS)
            sp.dma_start(ident[:, :], eye).then_inc(order_loaded, 16)
            sp.dma_start(to_score[:, :], to_score_in).then_inc(order_loaded, 16)
            with sp.Fori(1, TILES // 2) as i:
                for slot in range(2):
                    load_a(2 * i + slot)
                    sp.wait_ge(x_added, 2 * i + slot - 1)
                    sp.dma_start(resid[:, slot], x[2 * i + slot]).then_inc(x_loaded[slot], 16)

            sp.wait_ge(a_ready, AC * TILES)

            def load_group(i, slot, again):
                g = 2 * i + slot
                if again:
                    sp.wait_ge(g_transposed, HALVES * (g - 1))
                    sp.wait_ge(c_multiplied, g - 1)
                for s in range(2):
                    sp.wait_ge(x1_stored[s], 16 * GT // 2 * (g + 1))
                sp.dma_start(x1_group[:, slot], x1_dram[bass.ds(GT * g, GT)].rearrange("i p d -> p i d")
                             ).then_inc(g_loaded[slot], 16)

            def store_z(i, slot):
                g = 2 * i + slot
                hold(sp, "sync", zv_ready, 4 * g + HALVES)
                for k in range(GT):
                    sp.dma_start(z_dram[GT * g + k].rearrange("p s h n -> p (s h) n"),
                                 z_stage[:, slot].bitcast(F32).rearrange("p s h n -> p (s h) n")[:, :, k * P:(k + 1) * P]
                                 ).then_inc(z_stored[slot], 16)

            load_group(0, 0, False)
            load_group(0, 1, False)
            with sp.Fori(0, GROUPS // 2 - 1) as i:
                for slot in range(2):
                    load_group(i + 1, slot, True)
                    store_z(i, slot)

            def load_adj(t, c):
                sp.dma_start(adj_ring[:, c % (SC - 1)], adj[t][:, bass.ds(c * SCW, SCW)]
                             ).then_inc(adj_loaded[c % (SC - 1)], 16)

            load_adj(0, 0)
            load_adj(0, 1)
            for slot in range(2):
                sp.wait_ge(z_stored[slot], 16 * GT)
            for slot in range(2):
                sp.dma_start(z_tile[:, slot].bitcast(F32), z_dram[slot]).then_inc(z_loaded[slot], 16)
            sp.wait_ge(x_added, TILES)
            for slot in range(2):
                sp.wait_ge(x1b_stored[slot], 16 * TILES // 2)
            for slot in range(2):
                sp.dma_start(resid[:, slot], x1b_dram[slot]).then_inc(x1b_loaded[slot], 16)
            store_z(GROUPS // 2 - 1, 0)
            store_z(GROUPS // 2 - 1, 1)
            load_adj(0, 2)
            for slot in range(2):
                sp.wait_ge(z_stored[slot], 16 * GT * GROUPS // 2)

            def feed(i, slot, before, last):
                t = 2 * i + slot
                sp.wait_ge(s_ready, SC * t + 1)
                load_adj(t, SC - 1)
                if not last:
                    if before >= 1:
                        sp.wait_ge(s_product, SC * t)
                        sp.dma_start(z_tile[:, 1 - slot].bitcast(F32), z_dram[t + 1]
                                     ).then_inc(z_loaded[1 - slot], 16)
                    for c in (1, 2, 0):
                        hold(sp, "sync", s_ready, SC * t + (c + 1 if c else SC))
                        load_adj(t + 1, c)
                for a in range(QUADS):
                    if a == 0 and before >= 1:
                        sp.wait_ge(pT_raw, PC * t)
                    sp.wait_ge(p_ready, SC * t + a + 1)
                    sp.dma_start(dealt[a * S:(a + 1) * S], scores[:, a * QW:(a + 1) * QW]).then_inc(p_dealt[a], 16)
                if before >= 2:
                    sp.wait_ge(o_read, t - 1)
                    sp.dma_start(resid[:, slot], x1b_dram[t]).then_inc(x1b_loaded[slot], 16)

            feed(0, 0, 0, False)
            feed(0, 1, 1, False)
            with sp.Fori(1, TILES // 2 - 1) as i:
                feed(i, 0, 2, False)
                feed(i, 1, 2, False)
            feed(TILES // 2 - 1, 0, 2, False)
            feed(TILES // 2 - 1, 1, 2, True)
            sp.wait_ge(ln_done, 2 * TILES)
            sp.dma_start(out[TILES - 1], normed[:, 1, :]).then_inc(last_stored, 16)
            sp.wait_ge(last_stored, 16)

        @block.tensor
        def _(pe):
            def three_passes(bank, left, right, first, last):
                pe.matmul(bank, left(HI), right(HI), start=first, stop=False)
                pe.matmul(bank, left(HI), right(LO), start=False, stop=False)
                return pe.matmul(bank, left(LO), right(HI), start=False, stop=last)

            pe.wait_ge(w0_ready, 1)

            def y_group(i, slot, again):
                g = 2 * i + slot
                for pair in range(2):
                    bank = s_bank[2 * slot + pair]
                    if again:
                        pe.wait_ge(y_ready, 2 * (g - 2) + pair + 1)
                    for k in range(2):
                        rows = slice((2 * pair + k) * P, (2 * pair + k + 1) * P)
                        for h in range(HALVES):
                            if pair == 0 and k == 0:
                                pe.wait_ge(x0_split, HALVES * g + h + 1)
                            done = three_passes(bank[:, k * D:(k + 1) * D],
                                                lambda part: xT_split[:, slot, part, h, rows],
                                                lambda part: w0_split[:, part, h, :],
                                                h == 0, h == HALVES - 1)
                    done.then_inc(y_product, 1)

            y_group(0, 0, False)
            y_group(0, 1, False)
            with pe.Fori(1, GROUPS // 2) as i:
                y_group(i, 0, True)
                y_group(i, 1, True)

            def over_outputs(bank, left, right):
                for o in range(HALVES):
                    done = pe.matmul(bank, left(o), right(o), start=(o == 0), stop=(o == HALVES - 1))
                return done

            wq_raw, wk_raw = w_raw[:, 1], w_raw[:, 2]
            pe.wait_ge(w_loaded, 48)
            pe.wait_ge(const_loaded, 80)
            for h in range(HALVES):
                feats = slice(h * P, (h + 1) * P)
                over_outputs(t_bank[h][:, 0:D], lambda o: wq_raw[:, o, feats], lambda o: wk_raw[:, o, :])
                over_outputs(t_bank[1][:, D + h:D + h + 1], lambda o: wk_raw[:, o, feats],
                             lambda o: bq_col[:, o:o + 1])
            over_outputs(t_bank[0][:, D:2 * D], lambda o: bk_col[:, o:o + 1].broadcast_to([P, P]),
                         lambda o: wq_raw[:, o, :])
            over_outputs(t_bank[1][:, D + 2:D + 3], lambda o: bk_col[:, o:o + 1].broadcast_to([P, P]),
                         lambda o: bq_col[:, o:o + 1]).then_inc(m_product, 1)

            def aggregate(t, slot, again, chunks=range(AC), first=False):
                if again:
                    pe.wait_ge(agg_read, t - 1)
                for c in chunks:
                    if first:
                        pe.wait_ge(y_ready, 2 * GROUPS * (c + 1) // AC)
                    pe.wait_ge(a_ready, AC * t + c + 1)
                    for j in range(JA):
                        jt = c * JA + j
                        cols = slice(j * P, (j + 1) * P)
                        pe.matmul(o_bank[slot][:, :], a_split[:, slot, c, HI, cols], rhs_split[:, jt, :, :],
                                  start=(jt == 0), stop=False)
                        done = pe.matmul(o_bank[slot][:, D:2 * D], a_split[:, slot, c, LO, cols],
                                         rhs_split[:, jt, HI, :], start=False, stop=(jt == TILES - 1))
                    done.then_inc(a_used, 1)

            aggregate(0, 0, False, first=True)
            aggregate(1, 1, False)
            with pe.Fori(1, TILES // 2 - 1) as i:
                aggregate(2 * i, 0, True)
                aggregate(2 * i + 1, 1, True)
            aggregate(TILES - 2, 0, True)
            aggregate(TILES - 1, 1, True, range(AC // 2))

            pe.wait_ge(order_loaded, 32)
            pe.wait_ge(w_ready, 3)
            pe.wait_ge(m_terms, 1)

            def transpose_group(i, slot, again):
                g = 2 * i + slot
                pe.wait_ge(g_loaded[slot], 16 * (i + 1))
                for h in range(HALVES):
                    if again:
                        pe.wait_ge(g_split, HALVES * (g - 1) + h + 1)
                    for k in range(GT):
                        done = pe.transpose(t_bank[h][:, k * P:(k + 1) * P],
                                            x1_group[:, slot, k, h * P:(h + 1) * P], ident[:, :])
                    done.then_inc(g_transposed, 1)

            def project_z(i, slot, again, banks=s_bank):
                g = 2 * i + slot
                for half in range(HALVES):
                    if again:
                        pe.wait_ge(zv_ready, 4 * (g - 1) + half + 1)
                    feats = slice(half * P, (half + 1) * P)
                    for h in range(HALVES):
                        if half == 0:
                            pe.wait_ge(g_split, HALVES * g + h + 1)
                        done = three_passes(banks[half],
                                            lambda part: w_split[:, 0, part, h, feats],
                                            lambda part: x1T_split[:, h, part, g * BANK:(g + 1) * BANK],
                                            h == 0, h == HALVES - 1)
                    done.then_inc(zv_product, 1)

            def project_v(i, slot, again, banks):
                g = 2 * i + slot
                for pair in range(2):
                    if again:
                        pe.wait_ge(zv_ready, 4 * (g - 1) + HALVES + pair + 1)
                    for k in range(2):
                        for h in range(HALVES):
                            rows = slice((GT * g + 2 * pair + k) * P, (GT * g + 2 * pair + k + 1) * P)
                            done = three_passes(banks[pair][:, k * D:(k + 1) * D],
                                                lambda part: x1T_split[:, h, part, rows],
                                                lambda part: w_split[:, 1, part, h, :],
                                                h == 0, h == HALVES - 1)
                    done.then_inc(zv_product, 1)

            def group(i, slot, again):
                project_z(i, slot, again)
                transpose_group(i + slot, 1 - slot, True)
                project_v(i, slot, again, s_bank[2:])

            transpose_group(0, 0, False)
            aggregate(TILES - 1, 1, False, range(AC // 2, AC))
            for g in range(GROUPS - 1):
                group(g // 2, g % 2, g >= 1)
            pe.wait_ge(agg_read, TILES)
            project_z(GROUPS // 2 - 1, 1, False, o_bank)

            def score(i, slot, again, chunks=range(SC)):
                t = 2 * i + slot
                pe.wait_ge(z_loaded[slot], 16 * (i + 1))
                for c in chunks:
                    if again or c >= 2:
                        pe.wait_ge(s_ready, SC * t + c - 1)
                    for b in range(2):
                        tiles = slice(b * TILES // 2, (b + 1) * TILES // 2)
                        for h in range(HALVES):
                            done = three_passes(s_bank[2 * (c % 2) + b],
                                                lambda part: z_tile[:, slot, part, h, :],
                                                lambda part: x1T_split[:, h, part, :].rearrange(
                                                    "p (w a j) -> p a w j", a=QUADS, j=S)[:, c, tiles, :],
                                                h == 0, h == HALVES - 1)
                    done.then_inc(s_product, 1)

            def move_sums(t, slot, again):
                pe.wait_ge(p_ready, SC * (t + 1))
                if again:
                    pe.wait_ge(sum_found, t - 1)
                pe.matmul(t_bank[slot][:, 0:SC], to_tile[:, :], row_sum_of[:, slot, :],
                          start=True, stop=True).then_inc(sum_moved, 1)

            def attend(t, slot, again):
                if again:
                    pe.wait_ge(o_read, t - 1)
                for c in range(HC):
                    pe.wait_ge(pT_ready, HC * t + c + 1)
                    for k in range(GT):
                        jt = c * GT + k
                        pe.matmul(o_bank[slot][:, :], pT_split[:, c % 4, HI, k, :], rhs_split[:, jt, :, :],
                                  start=(jt == 0), stop=False)
                        done = pe.matmul(o_bank[slot][:, D:2 * D], pT_split[:, c % 4, LO, k, :],
                                         rhs_split[:, jt, HI, :], start=False, stop=(jt == TILES - 1))
                    done.then_inc(pv_done, 1)

            pe.wait_ge(zv_ready, 4 * (GROUPS - 1))
            score(0, 0, False)
            pe.wait_ge(c_summed, GROUPS)
            pe.matmul(t_bank[1][:, SC:SC + TILES], to_score[:, :], c_raw[:, :], start=True, stop=True
                      ).then_inc(c_moved, 1)
            score(0, 1, True, range(SC // 2))
            pe.wait_ge(zv_ready, 4 * (GROUPS - 1) + HALVES)
            project_v(GROUPS // 2 - 1, 1, False, o_bank)
            score(0, 1, True, range(SC // 2, SC))
            move_sums(0, 0, False)
            pe.wait_ge(zv_ready, 4 * GROUPS)
            attend(0, 0, False)
            score(1, 0, True)
            move_sums(1, 1, False)
            attend(1, 1, False)

            def step(i, slot):
                t = 2 * i + slot
                move_sums(t, slot, True)
                score(i + slot, 1 - slot, True)
                attend(t, slot, True)

            with pe.Fori(1, TILES // 2 - 1) as i:
                step(i, 0)
                step(i, 1)
            step(TILES // 2 - 1, 0)
            move_sums(TILES - 1, 1, True)
            attend(TILES - 1, 1, True)

        @block.scalar
        def _(act):
            act.wait_ge(w0_loaded, 16)
            act.activation(w0_split[:, HI], w_raw[:, 0], ACT.Copy).then_inc(w0_hi, 1)

            def y_group(i, slot, again):
                g = 2 * i + slot
                act.wait_ge(x0_loaded[slot], 16 * (i + 1))
                if again:
                    act.wait_ge(y_product, 2 * (g - 1))
                for h in range(HALVES):
                    act.activation(xT_split[:, slot, HI, h], x0_raw[:, g, h], ACT.Copy).then_inc(x0_hi, 1)

            def y_rows(i, slot, pairs):
                for pair in pairs:
                    act.wait_ge(y_product, 2 * (2 * i + slot) + pair + 1)
                    act.activation(rhs_split[:, bass.ds(GT * (2 * i + slot) + 2 * pair, 2), HI, :],
                                   s_bank[2 * slot + pair].rearrange("p (k d) -> p k d", k=2),
                                   ACT.Copy).then_inc(y_hi, 1)

            y_group(0, 0, False)
            y_group(0, 1, False)
            with act.Fori(1, GROUPS // 2) as i:
                for slot in range(2):
                    y_rows(i - 1, slot, (0,))
                    y_group(i, slot, True)
                    y_rows(i - 1, slot, (1,))

            def a_tile(i, slot, again):
                t = 2 * i + slot
                for c in range(AC):
                    act.wait_ge(a_loaded[c], 16 * (t + 1))
                    if again:
                        act.wait_ge(a_used, AC * (t - 2) + c + 1)
                    act.activation(a_split[:, slot, c, HI], a_raw[:, c], ACT.Copy).then_inc(a_hi, 1)

            a_tile(0, 0, False)
            for slot in range(2):
                y_rows(GROUPS // 2 - 1, slot, range(2))
            act.wait_ge(x0_split, HALVES * GROUPS)
            a_tile(0, 1, False)
            act.wait_ge(m_product, 1)
            for h in range(HALVES):
                act.activation(w_split[:, 0, HI, h], t_bank[h][:, 0:D], ACT.Copy, scale=HALF_SCALE
                               ).then_inc(w_hi, 1)
            act.activation(w_split[:, 1, HI], w_raw[:, 3], ACT.Copy).then_inc(w_hi, 1)
            with act.Fori(1, TILES // 2) as i:
                a_tile(i, 0, True)
                a_tile(i, 1, True)

            def group_hi(i, slot):
                g = 2 * i + slot
                for h in range(HALVES):
                    act.wait_ge(g_transposed, HALVES * g + h + 1)
                    act.activation(x1T_split[:, h, HI, bass.ds(g * BANK, BANK)], t_bank[h][:, :], ACT.Copy
                                   ).then_inc(g_hi, 1)

            def z_hi(i, slot, again, banks=s_bank):
                g = 2 * i + slot
                for half in range(HALVES):
                    act.wait_ge(zv_product, 4 * g + half + 1)
                    if again:
                        act.wait_ge(z_stored[slot], 16 * GT * i)
                    act.activation(z_raw[:, half, :].rearrange("p (w i s) -> p s w i", w=GT, s=QUADS),
                                   banks[half].rearrange("p (w s i) -> p s w i", w=GT, s=QUADS),
                                   ACT.Identity, bias=bz_col[:, half:half + 1]).then_inc(z_biased, 1)
                    act.wait_ge(z_biased, HALVES * g + half + 1)
                    act.activation(z_stage[:, slot, HI, half], z_raw[:, half, :], ACT.Copy).then_inc(zv_hi, 1)

            def v_hi(i, slot, banks):
                g = 2 * i + slot
                for pair in range(2):
                    act.wait_ge(zv_product, 4 * g + HALVES + pair + 1)
                    act.activation(rhs_split[:, bass.ds(GT * g + 2 * pair, 2), HI, :],
                                   banks[pair].rearrange("p (k d) -> p k d", k=2),
                                   ACT.Copy).then_inc(zv_hi, 1)

            def group(i, slot, again):
                z_hi(i, slot, again)
                group_hi(i + slot, 1 - slot)
                v_hi(i, slot, s_bank[2:])

            act.wait_ge(a_used, AC * (TILES - 1) + AC // 2)
            act.wait_ge(m_terms, 1)
            group_hi(0, 0)
            group(0, 0, False)
            group(0, 1, False)
            with act.Fori(1, GROUPS // 2 - 1) as i:
                group(i, 0, True)
                group(i, 1, True)
            group(GROUPS // 2 - 1, 0, True)
            z_hi(GROUPS // 2 - 1, 1, True, o_bank)

            def exp(t, slot, c):
                if c == 0:
                    act.wait_ge(max_ready, t + 1)
                s = scores[:, c * SCW:(c + 1) * SCW]
                act.activation(s, s, ACT.Exp, bias=exp_bias[:, slot, :], scale=2.0,
                               accum_out=row_sum_of[:, slot, c:c + 1]).then_inc(p_ready, 1)

            def pT_hi_part(t, c, again):
                act.wait_ge(pT_raw, PC * t + c // 2 + 1)
                if again or c >= 4:
                    act.wait_ge(pv_done, HC * t + c - 3)
                act.activation(pT_split[:, c % 4, HI], pT[:, c // 2 % 2, c % 2 * GT:(c % 2 + 1) * GT],
                               ACT.Copy).then_inc(pT_hi, 1)

            def step(t, slot, before, last):
                for c in range(4):
                    pT_hi_part(t, c, before >= 1)
                pT_hi_part(t, 4, True)
                for c in range(SC):
                    if not last:
                        exp(t + 1, 1 - slot, c)
                    if c == 1:
                        pT_hi_part(t, 5, True)
                        pT_hi_part(t, 6, True)
                    if c == 2:
                        pT_hi_part(t, 7, True)

            for c in range(SC):
                exp(0, 0, c)
            v_hi(GROUPS // 2 - 1, 1, o_bank)
            step(0, 0, 0, False)
            step(1, 1, 1, False)
            with act.Fori(1, TILES // 2 - 1) as i:
                step(2 * i, 0, 2, False)
                step(2 * i + 1, 1, 2, False)
            step(TILES - 2, 0, 2, False)
            step(TILES - 1, 1, 2, True)

        @block.vector
        def _(dve):
            def norm_stats(n, slot, again):
                dve.bn_stats(stats[:, :], acc[:, slot, :]).then_inc(ln_stats, 1)
                if again:
                    dve.wait_ge(ln_done, n - 1)
                hold(dve, "vector", ln_stats, n + 1)
                dve.bn_aggr(mean_var[:, slot, :], stats[:, :]).then_inc(ln_mean, 1)
                dve.wait_ge(ln_mean, n + 1)
                dve.tensor_scalar(var_eps[:, slot, :], mean_var[:, slot, 1:2], EPS, None, ALU.add).then_inc(ln_eps, 1)
                dve.wait_ge(ln_eps, n + 1)
                dve.tensor_scalar(half_bits[:, :].bitcast(I32), var_eps[:, slot, :].bitcast(I32), 1, None,
                                  ALU.logical_shift_right).then_inc(ln_shifted, 1)
                dve.wait_ge(ln_shifted, n + 1)
                dve.tensor_scalar(guess[:, slot, :].bitcast(I32), half_bits[:, :].bitcast(I32), -1.0,
                                  float(RSQRT_MAGIC), ALU.mult, ALU.add).then_inc(ln_seed, 1)

            def lo_part(out, whole, hi):
                return dve.tensor_tensor(out, whole, hi.bitcast(F32), ALU.subtract)

            dve.wait_ge(w0_hi, 1)
            lo_part(w0_split[:, LO], w_raw[:, 0], w0_split[:, HI]).then_inc(w0_ready, 1)

            def y_group(i, slot):
                g = 2 * i + slot
                for h in range(HALVES):
                    dve.wait_ge(x0_hi, HALVES * g + h + 1)
                    lo_part(xT_split[:, slot, LO, h], x0_raw[:, g, h], xT_split[:, slot, HI, h]).then_inc(x0_split, 1)

            def y_rows(i, slot, pairs):
                for pair in pairs:
                    dve.wait_ge(y_hi, 2 * (2 * i + slot) + pair + 1)
                    rows = bass.ds(GT * (2 * i + slot) + 2 * pair, 2)
                    lo_part(rhs_split[:, rows, LO, :],
                            s_bank[2 * slot + pair].rearrange("p (k d) -> p k d", k=2),
                            rhs_split[:, rows, HI, :]).then_inc(y_ready, 1)

            y_group(0, 0)
            y_group(0, 1)
            with dve.Fori(1, GROUPS // 2) as i:
                for slot in range(2):
                    y_rows(i - 1, slot, (0,))
                    y_group(i, slot)
                    y_rows(i - 1, slot, (1,))

            def a_tile(t, slot):
                for c in range(AC):
                    dve.wait_ge(a_hi, AC * t + c + 1)
                    lo_part(a_split[:, slot, c, LO], a_raw[:, c], a_split[:, slot, c, HI]).then_inc(a_ready, 1)

            def first_layer(i, slot, again):
                t = 2 * i + slot
                if again:
                    dve.wait_ge(ln_done, t - 1)
                dve.wait_ge(a_used, AC * (t + 1))
                dve.tensor_tensor(acc[:, slot, :], o_bank[slot][:, D:2 * D], b0_all[:, :], ALU.add
                                  ).then_inc(agg_biased, 1)
                dve.wait_ge(agg_biased, t + 1)
                dve.tensor_tensor(acc[:, slot, :], o_bank[slot][:, 0:D], acc[:, slot, :], ALU.add
                                  ).then_inc(agg_read, 1)
                dve.wait_ge(agg_read, t + 1)
                dve.wait_ge(x_loaded[slot], 16 * (i + 1))
                dve.scalar_tensor_tensor(out=acc[:, slot, :], in0=acc[:, slot, :], scalar=0.0,
                                         in1=resid[:, slot, :], op0=ALU.max, op1=ALU.add).then_inc(x_added, 1)
                dve.wait_ge(x_added, t + 1)
                norm_stats(t, slot, again)

            a_tile(0, 0)
            for slot in range(2):
                y_rows(GROUPS // 2 - 1, slot, range(2))
            a_tile(1, 1)
            for h in range(HALVES):
                dve.wait_ge(w_hi, h + 1)
                dve.scalar_tensor_tensor(out=w_split[:, 0, LO, h], in0=t_bank[h][:, 0:D], scalar=HALF_SCALE,
                                         in1=w_split[:, 0, HI, h].bitcast(F32),
                                         op0=ALU.mult, op1=ALU.subtract).then_inc(w_ready, 1)
            dve.wait_ge(w_hi, 3)
            lo_part(w_split[:, 1, LO], w_raw[:, 3], w_split[:, 1, HI]).then_inc(w_ready, 1)
            dve.tensor_scalar(bz_col[:, :], t_bank[1][:, D:D + HALVES], HALF_SCALE, None, ALU.mult)
            dve.tensor_scalar(c_const[:, :], t_bank[1][:, D + 2:D + 3], SCALE, None, ALU.mult)
            dve.tensor_scalar(u_all[:, :], t_bank[0][:, D:2 * D], SCALE, None, ALU.mult).then_inc(m_terms, 1)
            first_layer(0, 0, False)
            a_tile(2, 0)
            first_layer(0, 1, False)
            a_tile(3, 1)
            with dve.Fori(1, TILES // 2 - 1) as i:
                first_layer(i, 0, True)
                a_tile(2 * i + 2, 0)
                first_layer(i, 1, True)
                a_tile(2 * i + 3, 1)
            first_layer(TILES // 2 - 1, 0, True)

            def group_lo(i, slot, first=False):
                g = 2 * i + slot
                for h in range(HALVES):
                    if first and h == HALVES - 1:
                        dve.wait_ge(a_used, AC * TILES)
                    dve.wait_ge(g_hi, HALVES * g + h + 1)
                    cols = bass.ds(g * BANK, BANK)
                    lo_part(x1T_split[:, h, LO, cols], t_bank[h][:, :], x1T_split[:, h, HI, cols]).then_inc(g_split, 1)

            def z_lo(i, slot):
                g = 2 * i + slot
                for half in range(HALVES):
                    dve.wait_ge(zv_hi, 4 * g + half + 1)
                    lo_part(z_stage[:, slot, LO, half], z_raw[:, half, :], z_stage[:, slot, HI, half]
                            ).then_inc(zv_ready, 1)

            def v_lo(i, slot, pair, banks):
                g = 2 * i + slot
                dve.wait_ge(zv_hi, 4 * g + HALVES + pair + 1)
                rows = bass.ds(GT * g + 2 * pair, 2)
                lo_part(rhs_split[:, rows, LO, :], banks[pair].rearrange("p (k d) -> p k d", k=2),
                        rhs_split[:, rows, HI, :]).then_inc(zv_ready, 1)

            def sum_c(i, slot):
                g = 2 * i + slot
                dve.wait_ge(c_multiplied, g + 1)
                dve.tensor_reduce(c_raw[:, bass.ds(GT * g, GT)], c_product[:, :, :], AX_X, ALU.add
                                  ).then_inc(c_summed, 1)

            def group(i, slot):
                z_lo(i, slot)
                group_lo(i + slot, 1 - slot)
                for pair in range(2):
                    v_lo(i, slot, pair, s_bank[2:])
                sum_c(i + slot, 1 - slot)

            sum_c(0, 0)
            dve.wait_ge(a_used, AC * (TILES - 1))
            group_lo(0, 0, True)
            first_layer(TILES // 2 - 1, 1, True)
            with dve.Fori(0, GROUPS // 2 - 1) as i:
                group(i, 0)
                group(i, 1)
            group(GROUPS // 2 - 1, 0)
            z_lo(GROUPS // 2 - 1, 1)

            def add_adj(i, slot, c, again):
                t = 2 * i + slot
                if c % (SC - 1) == 0:
                    dve.wait_ge(adj_loaded[0], 32 * t + (16 if c == 0 else 32))
                else:
                    dve.wait_ge(adj_loaded[c], 16 * (t + 1))
                if again:
                    dve.wait_ge(p_dealt[c], 16 * t)
                hold(dve, "vector", s_product, SC * t + c + 1)
                dve.tensor_tensor_reduce(out=scores[:, c * SCW:(c + 1) * SCW],
                                         in0=s_pair[c % 2].rearrange("p b n -> p (b n)"),
                                         in1=adj_ring[:, c % (SC - 1), :],
                                         scale=1.0, scalar=-3.0e38, op0=ALU.add, op1=ALU.max,
                                         accum_out=row_max_of[:, c:c + 1]).then_inc(s_ready, 1)

            def whole_max(t, slot):
                dve.wait_ge(s_ready, SC * (t + 1))
                dve.tensor_reduce(chunk_max[:, :], row_max_of[:, :], AX_X, ALU.max).then_inc(max_found, 1)
                dve.wait_ge(max_found, t + 1)
                c = c_all[:, t:t + 1] if isinstance(t, int) else c_all[:, bass.ds(t, 1)]
                dve.scalar_tensor_tensor(out=row_max[:, :], in0=chunk_max[:, :], scalar=2.0, in1=c,
                                         op0=ALU.mult, op1=ALU.add).then_inc(max_shifted, 1)
                dve.wait_ge(max_shifted, t + 1)
                dve.tensor_tensor(exp_bias[:, slot, :], c, row_max[:, :], ALU.subtract).then_inc(max_ready, 1)

            def transpose_p(t, c, again):
                if again or c >= 2:
                    dve.wait_ge(pT_ready, HC * t + 2 * c - 2)
                if c == 0:
                    for a in range(QUADS):
                        dve.wait_ge(p_dealt[a], 16 * (t + 1))
                dve.transpose(pT[:, c % 2].rearrange("p w (q i) -> p q w i", q=QUADS),
                              dealt[:, :, c * CT * S:(c + 1) * CT * S].rearrange("p q (w i) -> p q w i", i=S)
                              ).then_inc(pT_raw, 1)

            def pT_lo(t, c):
                dve.wait_ge(pT_hi, HC * t + c + 1)
                lo_part(pT_split[:, c % 4, LO], pT[:, c // 2 % 2, c % 2 * GT:(c % 2 + 1) * GT],
                        pT_split[:, c % 4, HI]).then_inc(pT_ready, 1)

            def invert_sum(t, slot):
                dve.wait_ge(sum_moved, t + 1)
                dve.tensor_reduce(row_sum[:, :], t_bank[slot][:, 0:SC], AX_X, ALU.add).then_inc(sum_found, 1)
                dve.wait_ge(sum_found, t + 1)
                dve.reciprocal(inv_sum[:, slot, :], row_sum[:, :]).then_inc(sum_inverted, 1)

            def residual(i, slot):
                t = 2 * i + slot
                dve.wait_ge(sum_inverted, t + 1)
                dve.wait_ge(ln_done, TILES + t - 1)
                dve.wait_ge(pv_done, HC * (t + 1))
                dve.wait_ge(x1b_loaded[slot], 16 * (i + 1))
                dve.scalar_tensor_tensor(out=acc[:, slot, :], in0=o_bank[slot][:, D:2 * D],
                                         scalar=inv_sum[:, slot, :], in1=resid[:, slot, :],
                                         op0=ALU.mult, op1=ALU.add).then_inc(o_half, 1)
                dve.wait_ge(o_half, t + 1)
                dve.scalar_tensor_tensor(out=acc[:, slot, :], in0=o_bank[slot][:, 0:D],
                                         scalar=inv_sum[:, slot, :], in1=acc[:, slot, :],
                                         op0=ALU.mult, op1=ALU.add).then_inc(o_read, 1)

            def residual_stats(i, slot):
                t = 2 * i + slot
                dve.wait_ge(o_read, t + 1)
                norm_stats(TILES + t, slot, True)

            def step(i, slot):
                t = 2 * i + slot
                behind, ahead = (i - 1 + slot, 1 - slot), (i + slot, 1 - slot)
                add_adj(*ahead, 0, True)
                transpose_p(t, 0, True)
                add_adj(*ahead, 1, True)
                transpose_p(t, 1, True)
                add_adj(*ahead, 2, True)
                transpose_p(t, 2, True)
                pT_lo(t, 2)
                add_adj(*ahead, 3, True)
                whole_max(t + 1, 1 - slot)
                pT_lo(t, 3)
                transpose_p(t, 3, True)
                pT_lo(t, 4)
                invert_sum(t, slot)
                pT_lo(t, 5)
                pT_lo(t, 6)
                residual(*behind)
                pT_lo(t, 7)
                residual_stats(*behind)

            for c in range(SC):
                if c == SC // 2:
                    dve.wait_ge(z_stored[0], 16 * GT * GROUPS // 2)
                add_adj(0, 0, c, False)
            dve.wait_ge(c_moved, 1)
            dve.tensor_scalar(c_all[:, :], t_bank[1][:, SC:SC + TILES], c_const[:, :], None, ALU.add
                              ).then_inc(c_ready, 1)
            dve.wait_ge(c_ready, 1)
            whole_max(0, 0)
            for pair in range(2):
                add_adj(0, 1, pair, True)
                v_lo(GROUPS // 2 - 1, 1, pair, o_bank)
            add_adj(0, 1, 2, True)
            for slot in range(2):
                dve.wait_ge(x1b_stored[slot], 16 * TILES // 2)
            transpose_p(0, 0, False)
            transpose_p(0, 1, False)
            add_adj(0, 1, 3, True)
            whole_max(1, 1)
            transpose_p(0, 2, True)
            pT_lo(0, 2)
            pT_lo(0, 3)
            transpose_p(0, 3, True)
            pT_lo(0, 4)
            invert_sum(0, 0)
            for c in range(5, HC):
                pT_lo(0, c)
            step(0, 1)
            with dve.Fori(1, TILES // 2 - 1) as i:
                step(i, 0)
                step(i, 1)
            step(TILES // 2 - 1, 0)
            transpose_p(TILES - 1, 0, True)
            for c in range(PC):
                if c == PC - 1:
                    invert_sum(TILES - 1, 1)
                    residual(TILES // 2 - 1, 0)
                pT_lo(TILES - 1, 2 * c)
                pT_lo(TILES - 1, 2 * c + 1)
                if c < PC - 1:
                    transpose_p(TILES - 1, c + 1, True)
            residual_stats(TILES // 2 - 1, 0)
            residual(TILES // 2 - 1, 1)
            residual_stats(TILES // 2 - 1, 1)

            v, r = var_eps[:, 1, :], guess[:, 1, :]
            dve.wait_ge(ln_done, 2 * TILES - 1)
            dve.wait_ge(ln_seed, 2 * TILES)
            dve.tensor_scalar(half_var[:, :], v, -0.5, None, ALU.mult).then_inc(last_newton, 1)
            for k in range(NEWTON_STEPS):
                dve.wait_ge(last_newton, 2 * k + 1)
                dve.scalar_tensor_tensor(out=newton_a[:, :], in0=r, scalar=half_var[:, :], in1=r,
                                         op0=ALU.mult, op1=ALU.mult).then_inc(last_newton, 1)
                dve.wait_ge(last_newton, 2 * k + 2)
                dve.scalar_tensor_tensor(out=rstd[:, :], in0=newton_a[:, :], scalar=1.5, in1=r,
                                         op0=ALU.add, op1=ALU.mult).then_inc(last_newton, 1)
                r = rstd[:, :]
            dve.wait_ge(last_newton, 2 * NEWTON_STEPS + 1)
            dve.wait_ge(out_stored[1], 16 * (TILES // 2 - 1))
            dve.tensor_scalar(normed[:, 1, :], acc[:, 1, :], mean_var[:, 1, 0:1], rstd[:, :],
                              ALU.subtract, ALU.mult).then_inc(ln_done, 1)

        @block.gpsimd
        def _(pool):
            pool.wait_ge(const_loaded, 80)

            def normalise(n, slot):
                hold(pool, "gpsimd", ln_seed, n + 1)
                r = guess[:, slot, :]
                for k in range(NEWTON_STEPS):
                    before = 4 * NEWTON_STEPS * n + 4 * k
                    pool.tensor_tensor(newton_a[:, :], r, r, ALU.mult).then_inc(ln_newton, 1)
                    pool.wait_ge(ln_newton, before + 1)
                    pool.tensor_tensor(newton_a[:, :], newton_a[:, :], var_eps[:, slot, :], ALU.mult
                                       ).then_inc(ln_newton, 1)
                    hold(pool, "gpsimd", ln_newton, before + 2)
                    pool.tensor_scalar(newton_a[:, :], newton_a[:, :], -0.5, 1.5, ALU.mult, ALU.add
                                       ).then_inc(ln_newton, 1)
                    pool.wait_ge(ln_newton, before + 3)
                    pool.tensor_tensor(rstd[:, :], r, newton_a[:, :], ALU.mult).then_inc(ln_newton, 1)
                    r = rstd[:, :]
                    if k < NEWTON_STEPS - 1:
                        pool.wait_ge(ln_newton, before + 4)
                hold(pool, "gpsimd", ln_newton, 4 * NEWTON_STEPS * (n + 1))
                pool.tensor_scalar(normed[:, slot, :], acc[:, slot, :], mean_var[:, slot, 0:1], rstd[:, :],
                                   ALU.subtract, ALU.mult).then_inc(ln_done, 1)

            def keep_x1(i, slot, again):
                t = 2 * i + slot
                if again:
                    pool.wait_ge(x1_stored[slot], 16 * i)
                    pool.wait_ge(x1b_stored[slot], 16 * i)
                normalise(t, slot)
                pool.wait_ge(ln_done, t + 1)
                pool.tensor_tensor(x1b[:, slot, :], normed[:, slot, :], bv_all[:, :], ALU.add).then_inc(x1b_ready, 1)
                pool.dma_start(x1_dram[t], normed[:, slot, :]).then_inc(x1_stored[slot], 16)
                hold(pool, "gpsimd", x1b_ready, t + 1)
                pool.dma_start(x1b_dram[t], x1b[:, slot, :]).then_inc(x1b_stored[slot], 16)

            def multiply_c(i, slot, again):
                g = 2 * i + slot
                pool.wait_ge(g_loaded[slot], 16 * (i + 1))
                if again:
                    pool.wait_ge(c_summed, g)
                pool.tensor_tensor(c_product[:, :, :], x1_group[:, slot],
                                   u_all[:, :].unsqueeze(1).broadcast_to([P, GT, D]), ALU.mult
                                   ).then_inc(c_multiplied, 1)

            keep_x1(0, 0, False)
            keep_x1(0, 1, False)
            with pool.Fori(1, TILES // 2 - 1) as i:
                keep_x1(i, 0, True)
                keep_x1(i, 1, True)
            pool.wait_ge(m_terms, 1)
            multiply_c(0, 0, False)
            keep_x1(TILES // 2 - 1, 0, True)
            multiply_c(0, 1, True)
            keep_x1(TILES // 2 - 1, 1, True)
            with pool.Fori(1, GROUPS // 2) as i:
                multiply_c(i, 0, True)
                multiply_c(i, 1, True)

            for slot in range(2):
                pool.wait_ge(x1_stored[slot], 16 * TILES // 2)

            def finish(i, slot, again):
                t = 2 * i + slot
                if again:
                    pool.wait_ge(out_stored[slot], 16 * i)
                normalise(TILES + t, slot)
                hold(pool, "gpsimd", ln_done, TILES + t + 1)
                pool.dma_start(out[t], normed[:, slot, :]).then_inc(out_stored[slot], 16)

            def pT_lo_first(t):
                for c in range(POOL_PIECES):
                    pool.wait_ge(pT_hi, HC * t + c + 1)
                    pool.tensor_tensor(pT_split[:, c, LO], pT[:, 0, c * GT:(c + 1) * GT],
                                       pT_split[:, c, HI].bitcast(F32), ALU.subtract).then_inc(pT_ready, 1)

            pT_lo_first(0)
            pT_lo_first(1)
            finish(0, 0, False)
            pT_lo_first(2)
            finish(0, 1, False)
            pT_lo_first(3)
            finish(1, 0, True)
            with pool.Fori(2, TILES // 2 - 1) as i:
                pT_lo_first(2 * i)
                finish(i - 1, 1, True)
                pT_lo_first(2 * i + 1)
                finish(i, 0, True)
            pT_lo_first(TILES - 2)
            finish(TILES // 2 - 2, 1, True)
            finish(TILES // 2 - 1, 0, True)
            pool.wait_ge(out_stored[0], 16 * TILES // 2)
            pool.wait_ge(out_stored[1], 16 * (TILES // 2 - 1))


def kernel(x, adj, L0_gnn_W, L0_gnn_b, L1_gnn_Wq, L1_gnn_bq, L1_gnn_Wk, L1_gnn_bk, L1_gnn_Wv, L1_gnn_bv):
    import numpy as np
    import concourse.bacc as bacc
    from concourse.bass_utils import run_bass_kernel_spmd

    def tile_order(a):
        a = np.asarray(a)
        return a.reshape(QUADS, TILES, S, -1).transpose(1, 0, 2, 3).reshape(a.shape)

    def score_order(a):
        return a.reshape(TILES, QUADS, S, -1).transpose(0, 2, 1, 3).reshape(a.shape)

    x, adj = tile_order(x), tile_order(adj)
    adj_tiled = tile_order(adj.T).T

    def outputs_first(w):
        return np.ascontiguousarray(np.asarray(w).reshape(HALVES, P, D).transpose(1, 0, 2))

    def features_first(w):
        return np.ascontiguousarray(np.asarray(w).T.reshape(HALVES, P, D).transpose(1, 0, 2))

    def column(b):
        return np.ascontiguousarray(np.asarray(b).reshape(HALVES, P).T)

    to_tile = score_order(np.tile(np.eye(P, dtype=np.float32), (TILES, 1)))[:P].copy()
    arrays = {
        "xT": np.ascontiguousarray(x.reshape(GROUPS, BANK, HALVES, P).transpose(0, 3, 2, 1)),
        "x": np.ascontiguousarray(x.reshape(TILES, P, D)),
        "adjT": np.ascontiguousarray(
            adj_tiled.reshape(TILES, P, AC, JA, P).transpose(0, 4, 2, 3, 1)).reshape(TILES, P, AC, ACW),
        "adj": np.ascontiguousarray(score_order(adj)).reshape(TILES, P, N),
        "w0T": features_first(L0_gnn_W),
        "wq": outputs_first(L1_gnn_Wq),
        "wk": outputs_first(L1_gnn_Wk),
        "wvT": features_first(L1_gnn_Wv),
        "b0": np.ascontiguousarray(L0_gnn_b),
        "bq": column(L1_gnn_bq),
        "bk": column(L1_gnn_bk),
        "bv": np.ascontiguousarray(L1_gnn_bv),
        "eye": np.eye(P, dtype=np.float32),
        "to_tile": to_tile,
        "to_score": np.ascontiguousarray(to_tile.T),
    }
    nc = bacc.Bacc("TRN2", target_bir_lowering=False, num_devices=1)
    args = [nc.dram_tensor(f"in_{name}", a.shape, mybir.dt.from_np(a.dtype), kind="ExternalInput").ap()
            for name, a in arrays.items()]
    out = nc.dram_tensor("out", (TILES, P, D), F32, kind="ExternalOutput").ap()
    two_layers(nc, *args, out)
    r = run_bass_kernel_spmd(nc, [{f"in_{name}": a for name, a in arrays.items()}], core_ids=[0])
    return np.ascontiguousarray(r.results[0]["out"].reshape(TILES, QUADS, S, D).transpose(1, 0, 2, 3)).reshape(N, D)
```
